# Optimizing a Trainium2 kernel written in Bass

```python
import numpy as np
import jax
import jax.numpy as jnp

def _softmax(x, axis=-1):
    return jax.nn.softmax(x, axis=axis)

def _gelu(x):
    return jax.nn.gelu(x, approximate=True)

def _silu(x):
    return jax.nn.silu(x)

def _sigmoid(x):
    return jax.nn.sigmoid(x)

def _layernorm(x, axis=-1, eps=1e-05):
    m = jnp.mean(x, axis=axis, keepdims=True)
    v = jnp.var(x, axis=axis, keepdims=True)
    return (x - m) / jnp.sqrt(v + eps)

def _scatter_add(tgt, idx, src, axis=0):
    return tgt.at[idx].add(src)

def _segment_sum(src, seg, n):
    return jax.ops.segment_sum(src, seg, n)
kernel_name = 'mk_xattn_ffn_d1_seqx_r8_5181b5'

def setup_inputs(seed: int=0):
    np.random.seed(seed)
    _w = jnp.asarray

    def _rec_inputs():
        import jax
        import jax.numpy as jnp
        _rk = jax.random.key(seed)
        x = 7.22e-05 + 1 * jax.random.normal(jax.random.fold_in(_rk, 1), (32, 128, 128), jnp.float32)
        _lenS = 128 - jax.random.randint(jax.random.fold_in(_rk, 7), (32,), 0, max(1, 128 // 4) + 1, jnp.int32)
        _lenS2 = 128 - jax.random.randint(jax.random.fold_in(_rk, 8), (32,), 0, max(1, 128 // 4) + 1, jnp.int32)
        _ctx_768P = jax.random.normal(jax.random.fold_in(_rk, 11), (32, 16, 96), jnp.float32)
        _ctx_768c = jax.random.dirichlet(jax.random.fold_in(_rk, 511), 0.3 * jnp.ones((16,), jnp.float32), (32, 128))
        _ctx_768t = jnp.einsum('bsk,bkd->bsd', _ctx_768c, _ctx_768P)
        _ctx_768t = _ctx_768t * jax.lax.rsqrt(jnp.mean(jnp.square(_ctx_768t)) + 1e-12) * 0.953939
        ctx_768 = -0.000191848 + 0.999787 * (_ctx_768t + 0.3 * jax.random.normal(jax.random.fold_in(_rk, 611), (32, 128, 96), jnp.float32))
        return (x, ctx_768)
    x, ctx_768 = _rec_inputs()

    def _L0_xattn_setup():
        import jax, jax.numpy as jnp
        import numpy as np
        NUM_HEADS = 16
        CLAMP = 10000.0
        key = jax.random.key(seed)
        ks = jax.random.split(key, 8)
        B, Nq, Nkv, Cq, Ckv = (4, 256, 256, 128, 96)
        s_q = 1.0 / np.sqrt(Cq)
        s_kv = 1.0 / np.sqrt(Ckv)
        return {'query': jax.random.normal(ks[0], (B, Nq, Cq), jnp.float32), 'key_value': jax.random.normal(ks[1], (B, Nkv, Ckv), jnp.float32), 'Wq': jax.random.normal(ks[2], (Cq, Cq), jnp.float32) * s_q, 'bq': jnp.zeros((Cq,), jnp.float32), 'Wk': jax.random.normal(ks[3], (Ckv, Cq), jnp.float32) * s_kv, 'bk': jnp.zeros((Cq,), jnp.float32), 'Wv': jax.random.normal(ks[4], (Ckv, Cq), jnp.float32) * s_kv, 'bv': jnp.zeros((Cq,), jnp.float32), 'Wo': jax.random.normal(ks[5], (Cq, Cq), jnp.float32) * s_q, 'bo': jnp.zeros((Cq,), jnp.float32)}
    _L0_xattn_all = _L0_xattn_setup()
    _L0_xattn_in = {k: v for k, v in _L0_xattn_all.items() if k in ('Wq', 'bq', 'Wk', 'bk', 'Wv', 'bv', 'Wo', 'bo')}
    del _L0_xattn_all

    def _L0_ffn_setup():
        import jax, jax.numpy as jnp
        import numpy as np
        B, S, H, E, K = (2, 128, 128, 8, 2)
        F = 4 * H
        key = jax.random.key(seed)
        ks = jax.random.split(key, 8)
        std = 0.02
        return {'x': jax.random.normal(ks[0], (B, S, H), jnp.float32), 'gate_w': jax.random.normal(ks[1], (E, H), jnp.float32) * (std / np.sqrt(H)), 'gate_bias': jnp.zeros((E,), jnp.float32), 'Wu': jax.random.normal(ks[2], (E, F, H), jnp.float32) * std, 'bu': jnp.zeros((E, F), jnp.float32), 'Wd': jax.random.normal(ks[3], (E, H, F), jnp.float32) * std, 'bd': jnp.zeros((E, H), jnp.float32), 'sWu': jax.random.normal(ks[4], (F, H), jnp.float32) * std, 'sbu': jnp.zeros((F,), jnp.float32), 'sWd': jax.random.normal(ks[5], (H, F), jnp.float32) * std, 'sbd': jnp.zeros((H,), jnp.float32)}
    _L0_ffn_all = _L0_ffn_setup()
    _L0_ffn_in = {k: v for k, v in _L0_ffn_all.items() if k in ('gate_w', 'gate_bias', 'Wu', 'bu', 'Wd', 'bd', 'sWu', 'sbu', 'sWd', 'sbd')}
    del _L0_ffn_all
    return {'x': x, 'ctx_768': ctx_768, 'L0_xattn_Wq': _L0_xattn_in['Wq'], 'L0_xattn_bq': _L0_xattn_in['bq'], 'L0_xattn_Wk': _L0_xattn_in['Wk'], 'L0_xattn_bk': _L0_xattn_in['bk'], 'L0_xattn_Wv': _L0_xattn_in['Wv'], 'L0_xattn_bv': _L0_xattn_in['bv'], 'L0_xattn_Wo': _L0_xattn_in['Wo'], 'L0_xattn_bo': _L0_xattn_in['bo'], 'L0_ffn_gate_w': _L0_ffn_in['gate_w'], 'L0_ffn_gate_bias': _L0_ffn_in['gate_bias'], 'L0_ffn_Wu': _L0_ffn_in['Wu'], 'L0_ffn_bu': _L0_ffn_in['bu'], 'L0_ffn_Wd': _L0_ffn_in['Wd'], 'L0_ffn_bd': _L0_ffn_in['bd'], 'L0_ffn_sWu': _L0_ffn_in['sWu'], 'L0_ffn_sbu': _L0_ffn_in['sbu'], 'L0_ffn_sWd': _L0_ffn_in['sWd'], 'L0_ffn_sbd': _L0_ffn_in['sbd']}

def reference(x, ctx_768, L0_xattn_Wq, L0_xattn_bq, L0_xattn_Wk, L0_xattn_bk, L0_xattn_Wv, L0_xattn_bv, L0_xattn_Wo, L0_xattn_bo, L0_ffn_gate_w, L0_ffn_gate_bias, L0_ffn_Wu, L0_ffn_bu, L0_ffn_Wd, L0_ffn_bd, L0_ffn_sWu, L0_ffn_sbu, L0_ffn_sWd, L0_ffn_sbd):
    import jax
    import jax.numpy as jnp

    def _L0_xattn_ref(query, key_value, Wq, bq, Wk, bk, Wv, bv, Wo, bo):
        import jax, jax.numpy as jnp
        import numpy as np
        NUM_HEADS = 16
        CLAMP = 10000.0
        B, Nq, Cq = query.shape
        Nkv = key_value.shape[1]
        H = NUM_HEADS
        D = Cq // H
        scale = D ** (-0.5)
        q = (query @ Wq + bq).reshape(B, Nq, H, D).transpose(0, 2, 1, 3)
        k = (key_value @ Wk + bk).reshape(B, Nkv, H, D).transpose(0, 2, 1, 3)
        v = (key_value @ Wv + bv).reshape(B, Nkv, H, D).transpose(0, 2, 1, 3)
        attn = jnp.einsum('bhqd,bhkd->bhqk', q, k) * scale
        attn = jnp.clip(attn, -CLAMP, CLAMP)
        attn = jax.nn.softmax(attn, axis=-1)
        attn = jnp.where(jnp.any(jnp.isnan(attn)), jnp.asarray(1.0 / Nkv, attn.dtype), attn)
        x = jnp.einsum('bhqk,bhkd->bqhd', attn, v).reshape(B, Nq, Cq)
        return x @ Wo + bo

    def _L0_ffn_ref(x, gate_w, gate_bias, Wu, bu, Wd, bd, sWu, sbu, sWd, sbd):
        import jax, jax.numpy as jnp
        import numpy as np
        B, S, H, E, K = (2, 128, 128, 8, 2)
        F = 4 * H
        b, s, h = x.shape
        x_flat = x.reshape(-1, h)
        T = x_flat.shape[0]
        scores = jax.nn.sigmoid(x_flat @ gate_w.T + gate_bias)
        top_scores, top_idx = jax.lax.top_k(scores, K)
        top_scores = top_scores / (top_scores.sum(-1, keepdims=True) + 1e-06)
        w = jnp.zeros((T, E), x.dtype).at[jnp.arange(T)[:, None], top_idx].add(top_scores)
        h1 = jnp.einsum('th,efh->etf', x_flat, Wu) + bu[:, None, :]
        a1 = jax.nn.gelu(h1, approximate=False)
        y = jnp.einsum('etf,ehf->eth', a1, Wd) + bd[:, None, :]
        combined = jnp.einsum('te,eth->th', w, y)
        sh = jax.nn.gelu(x_flat @ sWu.T + sbu, approximate=False)
        shared = (sh @ sWd.T + sbd) * 0.1
        return (combined + shared).reshape(b, s, h)
    x = x + _L0_xattn_ref(_layernorm(x, axis=-1), ctx_768, L0_xattn_Wq, L0_xattn_bq, L0_xattn_Wk, L0_xattn_bk, L0_xattn_Wv, L0_xattn_bv, L0_xattn_Wo, L0_xattn_bo)
    x = x + _L0_ffn_ref(_layernorm(x, axis=-1), L0_ffn_gate_w, L0_ffn_gate_bias, L0_ffn_Wu, L0_ffn_bu, L0_ffn_Wd, L0_ffn_bd, L0_ffn_sWu, L0_ffn_sbu, L0_ffn_sWd, L0_ffn_sbd)
    return x

_drawn_inputs = setup_inputs


def setup_inputs(seed=0):
    import zlib

    import numpy as np

    out = dict(_drawn_inputs(seed))
    spreads = {'L0_xattn_bq': (0.0, 0.328),
     'L0_xattn_bk': (0.0, 0.8),
     'L0_xattn_bv': (0.0, 0.1),
     'L0_xattn_bo': (0.0, 0.1),
     'L0_ffn_gate_bias': (0.0, 0.1),
     'L0_ffn_bu': (0.0, 0.557),
     'L0_ffn_bd': (0.0, 0.1),
     'L0_ffn_sbu': (0.0, 0.8),
     'L0_ffn_sbd': (0.0, 0.8)}
    factors = {'L0_ffn_sWu': 8.0, 'L0_ffn_sWd': 8.0}
    for name, (base, spread) in spreads.items():
        noise = np.random.default_rng([zlib.crc32(name.encode()), seed]).standard_normal(out[name].shape)
        drawn = base * np.exp(spread * noise) if base else spread * noise
        out[name] = jnp.asarray(drawn.astype(out[name].dtype))
    for name, factor in factors.items():
        out[name] = (out[name] * factor).astype(out[name].dtype)
    return out
```

```python
from contextlib import ExitStack

import concourse.bass as bass
from concourse import mybir

F32 = mybir.dt.float32
I32 = mybir.dt.int32
U32 = mybir.dt.uint32
ALU = mybir.AluOpType
ACT = mybir.ActivationFunctionType
AX = mybir.AxisListType

P = 128
BATCHES = 32
CTX = 96
HEADS = 16
HD = P // HEADS
GROUPS = 4
PER = HEADS // GROUPS
CLAMP = 10000.0
EPS = 1e-5
TOKENS = BATCHES * P
EXPERTS = 8
TOPK = 2
CHUNKS = 4
HIDDEN = CHUNKS * P
TILES = TOKENS * TOPK // P + EXPERTS
UPW = HIDDEN + CHUNKS
DNW = HIDDEN + P
SG = 4
SGROUPS = BATCHES // SG
SW = SG * P
RING = 4
XCHUNKS = 4
LOOP_FROM, LOOP_TO = 6, 28
STEPS_FROM, STEPS_TO = -3, BATCHES + 3


def wait(eng, sem, count):
    if not isinstance(count, int) or count > 0:
        eng.wait_ge(sem, count)


def known(i, lo, hi):
    return not isinstance(i, int) or lo <= i < hi


def steps(eng, body, first, loop_from, loop_to, last, unroll):
    for i in range(first, loop_from):
        body(i, i, 0)
    with eng.Fori(0, (loop_to - loop_from) // unroll) as t:
        for u in range(unroll):
            body(t * unroll + (loop_from + u), loop_from + u, t)
    for i in range(loop_to, last):
        body(i, i, 0)


def xattn_moe(nc, dr, out):
    ctx_stack = ExitStack()
    with ctx_stack:
        def sb(name, shape, dt=F32):
            return ctx_stack.enter_context(nc.sbuf_tensor(name, shape, dt))

        def psum(name, width):
            return ctx_stack.enter_context(nc.psum_tensor(name, [P, width], F32))

        def sem(name):
            return ctx_stack.enter_context(nc.semaphore(name))

        wq, wk, wv, wo = sb("wq", [P, P]), sb("wk", [CTX, P]), sb("wv", [CTX, P]), sb("wo", [P, P])
        gate_w = sb("gate_w", [P, EXPERTS])
        bq, bk = sb("bq", [P, 1]), sb("bk", [P, 1])
        bv, bo = sb("bv", [P, P]), sb("bo", [P, P])
        gate_b = sb("gate_b", [P, EXPERTS])
        ident, tri, ones = sb("ident", [P, P]), sb("tri", [P, P]), sb("ones", [P, P])
        qmask, kmask = sb("qmask", [P, GROUPS]), sb("kmask", [P, PER])
        rank_w = sb("rank_w", [P, EXPERTS])
        tile_at = sb("tile_at", [P, TILES])
        up_w = sb("up_w", [P, EXPERTS * UPW])
        down_w = sb("down_w", [P, EXPERTS * DNW])
        s_up, s_upb, s_down = sb("s_up", [P, HIDDEN]), sb("s_upb", [P, CHUNKS]), sb("s_down", [P, HIDDEN])
        s_downb, s_downb01 = sb("s_downb", [P, P]), sb("s_downb01", [P, P])
        minus_half, eps = sb("minus_half", [P, 1]), sb("eps", [P, 1])
        zero = sb("zero", [P, P])

        x = sb("x", [P, TOKENS])
        xn2 = sb("xn2", [P, TOKENS])
        xn2t = sb("xn2t", [P, TOKENS])
        logits = sb("logits", [P, BATCHES * EXPERTS])

        def two(name, shape, dt=F32):
            return [sb(f"{name}{n}", shape, dt) for n in range(2)]

        ctxt = two("ctxt", [CTX, P])
        xn1, xn1t = two("xn1", [P, P]), two("xn1t", [P, P])
        stat1, mv1, ve1, rstd1 = two("stat1_", [P, 6]), two("mv1_", [P, 2]), two("ve1_", [P, 1]), two("rstd1_", [P, 1])
        stat2, mv2, ve2, rstd2 = two("stat2_", [P, 6]), two("mv2_", [P, 2]), two("ve2_", [P, 1]), two("rstd2_", [P, 1])
        km, qm = two("km", [P, PER * P]), two("qm", [P, GROUPS * P])
        val = two("val", [P, HEADS * P])
        clipped, probs = two("clipped", [P, HEADS * P]), two("probs", [P, HEADS * P])
        negmax, sums = two("negmax", [P, HEADS]), two("sums", [P, HEADS])
        recip, recipt = two("recip", [P, P]), two("recipt", [P, P])
        probst = two("probst", [P, PER * P])
        ot, xb = two("ot", [P, P]), two("xb", [P, P])
        xn2s, xn2ts = two("xn2s", [P, P]), two("xn2ts", [P, P])

        bank_s = psum("bank_s", GROUPS * 512)
        bank_t = [psum(f"bank_t{n}", 512) for n in range(2)]
        bank_a, bank_b = psum("bank_a", 512), psum("bank_b", 512)
        kv_k, kv_v, kv_q = bank_a[:, 0:P], bank_a[:, P:2 * P], bank_a[:, 2 * P:3 * P]
        proj_ps, gate_ps = bank_a[:, 0:P], bank_a[:, P:P + EXPERTS]
        xn1t_ps, xn2t_ps = bank_a[:, 0:P], bank_a[:, P:2 * P]
        ot_ps, recipt_ps = bank_b[:, 0:P], bank_b[:, P:2 * P]

        consts_in = sem("consts_in")
        ffn_in = sem("ffn_in")
        x_in = [sem(f"x_in{n}") for n in range(XCHUNKS)]
        ctx_in = [sem(f"ctx_in{n}") for n in range(2)]
        fills = sem("fills")
        zeroed = sem("zeroed")
        slots_zeroed = sem("slots_zeroed")
        stat1_done, mv1_done, ve1_done, rstd1_done = sem("stat1_done"), sem("mv1_done"), sem("ve1_done"), sem("rstd1_done")
        stat2_done, mv2_done, ve2_done, rstd2_done = sem("stat2_done"), sem("mv2_done"), sem("ve2_done"), sem("rstd2_done")
        xn1_done, xn1t_mm, xn1t_done = sem("xn1_done"), sem("xn1t_mm"), sem("xn1t_done")
        kvq_mm, v_done, km_done, qm_done = sem("kvq_mm"), sem("v_done"), sem("km_done"), sem("qm_done")
        scores_mm, clip_done, max_done = sem("scores_mm"), sem("clip_done"), sem("max_done")
        exp_done = sem("exp_done")
        probst_mm, probst_done, pv_mm = sem("probst_mm"), sem("probst_done"), sem("pv_mm")
        recip_done, recipt_mm, recipt_done, ot_done = sem("recip_done"), sem("recipt_mm"), sem("recipt_done"), sem("ot_done")
        proj_mm, xb_done, x1_done = sem("proj_mm"), sem("xb_done"), sem("x1_done")
        xn2_done, xn2t_mm, xn2t_done = sem("xn2_done"), sem("xn2t_mm"), sem("xn2t_done")
        gate_mm, gate_done = sem("gate_mm"), sem("gate_done")
        xn2_kept, xn2t_kept = sem("xn2_kept"), sem("xn2t_kept")

        sig_done, route = sem("sig_done"), sem("route")
        chosen, rank_mm, slots_done = sem("chosen"), sem("rank_mm"), sem("slots_done")
        scattered = sem("scattered")
        s_up_mm, s_gelu = sem("s_up_mm"), sem("s_gelu")
        s_down_mm, s_bias, s_added = sem("s_down_mm"), sem("s_bias"), sem("s_added")
        xs_in = [sem(f"xs_in{n}") for n in range(RING)]
        xst_mm, xst_done, up_w_done, down_w_done = sem("xst_mm"), sem("xst_done"), sem("up_w_done"), sem("down_w_done")
        up_mm, gelu_done, down_mm, y_done = sem("up_mm"), sem("gelu_done"), sem("down_mm"), sem("y_done")
        y_out = [sem(f"y_out{n}") for n in range(RING)]
        y_in = [sem(f"y_in{n}") for n in range(RING)]
        half_sum, summed = sem("half_sum"), sem("summed")
        stored = sem("stored")

        RE = BATCHES * EXPERTS
        sig, sig2, eq, sc = (sb(n, [P, RE]) for n in ("sig", "sig2", "eq", "sc"))
        oh = [sb(f"oh{k}", [P, RE]) for k in range(TOPK)]
        both, pre_a, pre_b, slot_of = (sb(n, [P, RE]) for n in ("both", "pre_a", "pre_b", "slot_of"))
        best = [sb(f"best{k}", [P, BATCHES]) for k in range(TOPK)]
        win, den, rden = (sb(n, [P, BATCHES]) for n in ("win", "den", "rden"))
        weight = [sb(f"weight{k}", [P, BATCHES]) for k in range(TOPK)]
        slot_f = [sb(f"slot_f{k}", [P, BATCHES]) for k in range(TOPK)]
        slot = [sb(f"slot{k}", [P, BATCHES], I32) for k in range(TOPK)]
        count, padded, base_a, base_b, ends = (sb(n, [P, EXPERTS]) for n in ("count", "padded", "base_a", "base_b", "ends"))
        count_i, count_j = sb("count_i", [P, EXPERTS], I32), sb("count_j", [P, EXPERTS], I32)
        passed = sb("passed", [P, TILES * EXPERTS])
        expert_f, expert_g = sb("expert_f", [P, TILES]), sb("expert_g", [P, TILES])
        expert = sb("expert", [P, TILES], I32)
        s_act = probs
        xs = [sb(f"xs{n}", [P, P]) for n in range(RING)]
        xst = two("xst", [P, P])
        st_up, st_down = two("st_up", [P, UPW]), two("st_down", [P, DNW])
        act = two("act", [P, HIDDEN])
        y = [sb(f"y{n}", [P, P]) for n in range(RING)]
        yg = [sb(f"yg{n}", [P, TOPK * P]) for n in range(RING)]
        part = two("part", [P, P])

        slots_x = nc.dram_tensor("slots_x", (TILES * P, P), F32).ap()
        slots_y = nc.dram_tensor("slots_y", (TILES * P, P), F32).ap()

        def tok(t, b, n=1):
            return t[:, bass.ds(b * P, n * P)] if not isinstance(b, int) else t[:, b * P:(b + n) * P]

        def by_e(t):
            return t[:, :].rearrange("p (t e) -> p t e", e=EXPERTS)

        consts = [(wq, "wq"), (wk, "wk"), (wv, "wv"), (wo, "wo"), (gate_w, "gate_w"), (bq, "bq"), (bk, "bk"),
                  (ident, "ident"), (tri, "tri"), (qmask, "qmask"), (kmask, "kmask")]
        rows = [(bv, "bv"), (bo, "bo"), (gate_b, "gate_b"), (rank_w, "rank_w"), (tile_at, "tile_at")]
        N_CONSTS = 16 * (len(consts) + len(rows))
        N_FFN = 16 * 7 + 16

        block = ctx_stack.enter_context(nc.Block())

        @block.sync
        def _(sp):
            xv = dr["x"].rearrange("b s c -> s b c")
            n = BATCHES // XCHUNKS

            def load_x(c):
                sp.dma_start(tok(x, c * n, n).rearrange("p (b c) -> p b c", c=P),
                             xv[:, c * n:(c + 1) * n, :]).then_inc(x_in[c], 16)

            def load_ctx(b, s, t):
                wait(sp, kvq_mm, b)
                src = dr["ctxt"][:, b * P:(b + 1) * P] if isinstance(b, int) else dr["ctxt"][:, bass.ds(b * P, P)]
                sp.dma_start(ctxt[s % 2][:, :], src).then_inc(ctx_in[s % 2], 16)

            load_x(0)
            for dst, name in consts:
                sp.dma_start(dst[:, :], dr[name]).then_inc(consts_in, 16)
            for dst, name in rows:
                sp.dma_start(dst[:, :], dr[name].partition_broadcast(P)).then_inc(consts_in, 16)
            load_ctx(0, 0, 0)
            load_ctx(1, 1, 0)
            for c in range(1, XCHUNKS):
                load_x(c)
            sp.dma_start(s_up[:, :], dr["s_up"]).then_inc(ffn_in, 16)
            sp.dma_start(s_down[:, :], dr["s_down"]).then_inc(ffn_in, 16)
            sp.dma_start(s_upb[:, :], dr["s_upb"]).then_inc(ffn_in, 16)
            sp.dma_start(s_downb[:, :], dr["s_downb"].partition_broadcast(P)).then_inc(ffn_in, 16)
            upv = up_w[:, :].rearrange("p (e w) -> p e w", w=UPW)
            dnv = down_w[:, :].rearrange("p (e w) -> p e w", w=DNW)
            sp.dma_start(upv[:, :, 0:HIDDEN], dr["up"]).then_inc(ffn_in, 16)
            sp.dma_start(upv[:, :, HIDDEN:UPW], dr["upb"]).then_inc(ffn_in, 16)
            sp.dma_start(dnv[:, :, 0:HIDDEN], dr["down"]).then_inc(ffn_in, 16)
            sp.dma_start(dnv[:, :, HIDDEN:DNW], dr["downb"].partition_broadcast(P)).then_inc(ffn_in, 16)
            sp.wait_ge(zeroed, 1)
            sp.dma_start(slots_x.rearrange("(t p) c -> p t c", p=P),
                         zero[:, :].unsqueeze(1).to_broadcast([P, TILES, P])).then_inc(slots_zeroed, 16)
            with sp.Fori(1, BATCHES // 2) as t:
                load_ctx(t * 2, 0, t)
                load_ctx(t * 2 + 1, 1, t)

            sp.wait_ge(scattered, 16 * TOPK * BATCHES)

            def slot_rows(ap, j):
                return ap[j * P:(j + 1) * P, :] if isinstance(j, int) else ap[bass.ds(j * P, P), :]

            def tile_io(j, s, t):
                if known(j, 0, TILES):
                    wait(sp, xst_mm, j - RING + 1)
                    sp.dma_start(xs[s % RING][:, :], slot_rows(slots_x, j)).then_inc(xs_in[s % RING], 16)
                b = j - RING
                if known(b, 0, TILES):
                    wait(sp, y_done, b + 1)
                    sp.dma_start(slot_rows(slots_y, b), y[s % RING][:, :]).then_inc(y_out[s % RING], 16)

            steps(sp, tile_io, 0, RING, TILES, TILES + RING, RING)

            ov = out.rearrange("b s c -> s b c")
            for g in range(SGROUPS):
                sp.wait_ge(summed, (g + 1) * SG)
                sp.dma_start(ov[:, g * SG:(g + 1) * SG, :],
                             tok(x, g * SG, SG).rearrange("p (b c) -> p b c", c=P)).then_inc(stored, 16)
            sp.wait_ge(stored, 16 * SGROUPS)

        @block.gpsimd
        def _(pool):
            nc.gpsimd.memset(minus_half[:, :], -0.5).then_inc(fills, 1)
            nc.gpsimd.memset(eps[:, :], EPS).then_inc(fills, 1)
            nc.gpsimd.memset(zero[:, :], 0.0).then_inc(zeroed, 1)
            nc.gpsimd.memset(ones[:, :], 1.0).then_inc(fills, 1)
            for v in val:
                nc.gpsimd.memset(v[:, :], 0.0).then_inc(fills, 1)
            pool.wait_ge(fills, 5)
            pool.wait_ge(consts_in, N_CONSTS)

            def rstd(b, mv, ve, out_, mv_done, ve_done, done, used, s):
                wait(pool, mv_done, b + 1)
                wait(pool, used, b - 1)
                nc.gpsimd.tensor_tensor(ve[s][:, :], mv[s][:, 1:2], eps[:, :], ALU.add).then_inc(ve_done, 1)
                wait(pool, ve_done, b + 1)
                nc.gpsimd.tensor_tensor(out_[s][:, :], ve[s][:, :], minus_half[:, :], ALU.pow).then_inc(done, 1)

            def step(i, s, t):
                if known(i + 3, 0, BATCHES):
                    rstd(i + 3, mv1, ve1, rstd1, mv1_done, ve1_done, rstd1_done, xn1_done, (s + 3) % 2)
                b = i - 1
                if known(b, 0, BATCHES):
                    wait(pool, x1_done, b - 1)
                    nc.gpsimd.tensor_tensor(xb[(s - 1) % 2][:, :], tok(x, b), bo[:, :], ALU.add).then_inc(xb_done, 1)
                if known(i - 3, 0, BATCHES):
                    rstd(i - 3, mv2, ve2, rstd2, mv2_done, ve2_done, rstd2_done, xn2_done, (s - 3) % 2)
                b, p = i - 3, (s - 3) % 2
                if known(b, 0, BATCHES):
                    wait(pool, xn2_done, b + 1)
                    nc.gpsimd.tensor_copy(tok(xn2, b), xn2s[p][:, :]).then_inc(xn2_kept, 1)
                    wait(pool, xn2t_done, b + 1)
                    nc.gpsimd.tensor_copy(tok(xn2t, b), xn2ts[p][:, :]).then_inc(xn2t_kept, 1)

            steps(pool, step, STEPS_FROM, LOOP_FROM, LOOP_TO, STEPS_TO, 2)

            pool.wait_ge(slots_zeroed, 16)
            pool.wait_ge(xn2_kept, BATCHES)
            pool.wait_ge(slots_done, 1)
            for t in range(BATCHES):
                for k in range(TOPK):
                    nc.gpsimd.indirect_dma_start(
                        out=slots_x, out_offset=bass.IndirectOffsetOnAxis(ap=slot[k][:, t:t + 1].bitcast(U32), axis=0),
                        in_=tok(xn2, t), in_offset=None).then_inc(scattered, 16)
            for n in range(RING):
                pool.wait_ge(y_out[n], 16 * (TILES // RING))
            for t in range(BATCHES):
                n = t % RING
                if t >= RING:
                    pool.wait_ge(summed, t - RING + 1)
                for k in range(TOPK):
                    nc.gpsimd.indirect_dma_start(
                        out=yg[n][:, k * P:(k + 1) * P], out_offset=None, in_=slots_y,
                        in_offset=bass.IndirectOffsetOnAxis(ap=slot[k][:, t:t + 1].bitcast(U32), axis=0),
                    ).then_inc(y_in[n], 16)

        @block.tensor
        def _(pe):
            mm, tr = nc.tensor.matmul, nc.tensor.transpose
            pe.wait_ge(consts_in, N_CONSTS)
            pe.wait_ge(fills, 5)

            def step(i, s, t):
                b, p = i + 1, (s + 1) % 2
                if known(b, 0, BATCHES) or known(i, 0, BATCHES):
                    wait(pe, qm_done, min(b, BATCHES) if isinstance(b, int) else b)
                    wait(pe, v_done, i)
                    wait(pe, x1_done, b - 3)
                    wait(pe, gate_done, b - 4)
                    wait(pe, xn1t_done, min(b + 1, BATCHES) if isinstance(b, int) else b + 1)
                if known(i, 0, BATCHES):
                    last = mm(kv_v, ctxt[s % 2][:, :], wv[:, :], start=True, stop=True)
                if known(b, 0, BATCHES):
                    pe.wait_ge(ctx_in[p], (t + (s + 1) // 2 + 1) * 16)
                    mm(kv_k, wk[:, :], ctxt[p][:, :], start=True, stop=True)
                    last = mm(kv_q, wq[:, :], xn1t[p][:, :], start=True, stop=True)
                if known(b, 0, BATCHES) or known(i, 0, BATCHES):
                    last.then_inc(kvq_mm, 1)
                b, p = i, s % 2
                if known(b, 0, BATCHES):
                    wait(pe, qm_done, b + 1)
                    wait(pe, clip_done, b)
                    for j in range(GROUPS):
                        last = mm(bank_s[:, j * 512:(j + 1) * 512], qm[p][:, j * P:(j + 1) * P], km[p][:, :],
                                  start=True, stop=True)
                    last.then_inc(scores_mm, 1)
                b, p = i - 1, (s - 1) % 2

                def turn(g):
                    wait(pe, exp_done, 4 * b + g + 1)
                    wait(pe, probst_done, 4 * b + g - 1)
                    for r in range(PER):
                        h = g * PER + r
                        last = tr(bank_t[g % 2][:, r * P:(r + 1) * P], probs[p][:, h * P:(h + 1) * P], ident[:, :])
                    last.then_inc(probst_mm, 1)

                def weigh(g):
                    wait(pe, probst_done, 4 * b + g + 1)
                    if g == 0:
                        wait(pe, v_done, b + 1)
                        wait(pe, ot_done, b)
                    for r in range(PER):
                        h = g * PER + r
                        last = mm(ot_ps, val[p][:, h * P:(h + 1) * P], probst[g % 2][:, r * P:(r + 1) * P],
                                  start=(h == 0), stop=(h == HEADS - 1))
                    last.then_inc(pv_mm, 1)

                if known(b, 0, BATCHES):
                    turn(0)
                    turn(1)
                if known(i + 2, 0, BATCHES) or known(i - 3, 0, BATCHES):
                    wait(pe, v_done, min(i + 1, BATCHES) if isinstance(i, int) else i + 1)
                    wait(pe, qm_done, min(i + 2, BATCHES) if isinstance(i, int) else i + 2)
                    if isinstance(i, int) and i >= BATCHES:
                        wait(pe, x1_done, i - 2)
                        wait(pe, gate_done, i - 3)
                if known(i - 3, 0, BATCHES):
                    wait(pe, xn2_done, i - 2)
                    tr(xn2t_ps, xn2s[(s - 3) % 2][:, :], ident[:, :]).then_inc(xn2t_mm, 1)
                if known(i + 2, 0, BATCHES):
                    wait(pe, xn1_done, i + 3)
                    tr(xn1t_ps, xn1[s % 2][:, :], ident[:, :]).then_inc(xn1t_mm, 1)
                if known(b, 0, BATCHES):
                    weigh(0)
                    turn(2)
                if known(i - 2, 0, BATCHES) or known(i - 3, 0, BATCHES):
                    wait(pe, xn1t_done, min(i + 3, BATCHES) if isinstance(i, int) else i + 3)
                    wait(pe, xn2t_done, i - 2)
                if known(i - 2, 0, BATCHES):
                    wait(pe, ot_done, i - 1)
                    mm(proj_ps, ot[s % 2][:, :], wo[:, :], start=True, stop=True).then_inc(proj_mm, 1)
                if known(i - 3, 0, BATCHES):
                    mm(gate_ps, xn2ts[(s - 3) % 2][:, :], gate_w[:, :], start=True, stop=True).then_inc(gate_mm, 1)
                if known(b, 0, BATCHES):
                    weigh(1)
                    turn(3)
                    weigh(2)
                    weigh(3)
                    wait(pe, recip_done, b + 1)
                    tr(recipt_ps, recip[p][:, :], ident[:, :]).then_inc(recipt_mm, 1)

            steps(pe, step, STEPS_FROM, LOOP_FROM, LOOP_TO, STEPS_TO, 2)

            pe.wait_ge(ffn_in, N_FFN)
            pe.wait_ge(clip_done, BATCHES)
            pe.wait_ge(xn2t_kept, BATCHES)
            pe.wait_ge(probst_done, 4 * BATCHES)
            pe.wait_ge(ot_done, BATCHES)

            def shared(g, s, t):
                if known(g, 0, SGROUPS):
                    for c in range(CHUNKS):
                        wait(pe, s_gelu, 4 * (g - 1) + c + 1)
                        mm(bank_s[:, c * 512:(c + 1) * 512], s_up[:, c * P:(c + 1) * P],
                           tok(xn2t, g * SG, SG), start=True, stop=True).then_inc(s_up_mm, 1)
                b, p = g - 1, (s - 1) % 2
                if known(b, 0, SGROUPS):
                    wait(pe, s_gelu, 4 * (b + 1))
                    wait(pe, s_added, b - 1)
                    for q in range(SG):
                        for c in range(CHUNKS):
                            last = mm(bank_t[p][:, q * P:(q + 1) * P], s_act[p][:, c * SW + q * P:c * SW + (q + 1) * P],
                                      s_down[:, c * P:(c + 1) * P], start=(c == 0), stop=(c == CHUNKS - 1))
                    last.then_inc(s_down_mm, 1)

            shared(0, 0, 0)
            pe.wait_ge(chosen, 1)
            pe.wait_ge(gate_done, BATCHES)
            mm(bank_a[:, 0:RE], tri[:, :], both[:, :], start=True, stop=True)
            mm(bank_b[:, 0:RE], ones[:, :], both[:, :], start=True, stop=True).then_inc(rank_mm, 1)
            steps(pe, shared, 1, 2, SGROUPS, SGROUPS + 1, 2)

            pe.wait_ge(slots_done, 1)
            pe.wait_ge(s_gelu, 4 * SGROUPS)
            pe.wait_ge(s_added, SGROUPS)

            def routed(j, s, t):
                b, p = j + 1, (s + 1) % 2
                if known(b, 0, TILES):
                    pe.wait_ge(xs_in[(s + 1) % RING], (t + (s + 1) // RING + 1) * 16)
                    wait(pe, xst_done, b - 1)
                    tr((bank_a, bank_b)[p][:, 0:P], xs[(s + 1) % RING][:, :], ident[:, :]).then_inc(xst_mm, 1)
                b, p = j, s % 2
                if known(b, 0, TILES):
                    wait(pe, xst_done, b + 1)
                    wait(pe, up_w_done, b + 1)
                    wait(pe, gelu_done, b - 1)
                    for c in range(CHUNKS):
                        last = mm(bank_s[:, p * 512 + c * P:p * 512 + (c + 1) * P], st_up[p][:, c * P:(c + 1) * P],
                                  xst[p][:, :], start=True, stop=True)
                    last.then_inc(up_mm, 1)
                b, p = j - 1, (s - 1) % 2
                if known(b, 0, TILES):
                    wait(pe, gelu_done, b + 1)
                    wait(pe, down_w_done, b + 1)
                    wait(pe, y_done, b - 1)
                    for c in range(CHUNKS):
                        last = mm(bank_t[p][:, 0:P], act[p][:, c * P:(c + 1) * P], st_down[p][:, c * P:(c + 1) * P],
                                  start=(c == 0), stop=(c == CHUNKS - 1))
                    last.then_inc(down_mm, 1)

            steps(pe, routed, -1, 3, TILES - 1, TILES + 1, RING)

        @block.scalar
        def _(sc_):
            act_ = nc.scalar.activation

            def step(i, s, t):
                b, p = i - 1, (s - 1) % 2
                if known(b, 0, BATCHES):
                    wait(sc_, max_done, b + 1)
                    wait(sc_, probst_mm, 4 * (b - 1))
                    wait(sc_, recip_done, b - 1)
                    for h in range(HEADS):
                        ins = act_(probs[p][:, h * P:(h + 1) * P], clipped[p][:, h * P:(h + 1) * P], ACT.Exp,
                                   bias=negmax[p][:, h:h + 1], accum_out=sums[p][:, h:h + 1])
                        if h % PER == PER - 1:
                            ins.then_inc(exp_done, 1)

                def evacuate(g):
                    wait(sc_, probst_mm, 4 * b + g + 1)
                    wait(sc_, pv_mm, 4 * b + g - 1)
                    nc.scalar.copy(probst[g % 2][:, :], bank_t[g % 2][:, :]).then_inc(probst_done, 1)

                if known(b, 0, BATCHES):
                    evacuate(0)
                    evacuate(1)
                if known(i + 2, 0, BATCHES):
                    wait(sc_, xn1t_mm, i + 3)
                if known(i - 3, 0, BATCHES):
                    wait(sc_, xn2t_mm, i - 2)
                    wait(sc_, gate_mm, i - 4)
                    wait(sc_, xn2t_kept, i - 4)
                    nc.scalar.copy(xn2ts[(s - 3) % 2][:, :], xn2t_ps).then_inc(xn2t_done, 1)
                if known(i + 2, 0, BATCHES):
                    wait(sc_, kvq_mm, i + 1)
                    nc.scalar.copy(xn1t[s % 2][:, :], xn1t_ps).then_inc(xn1t_done, 1)
                if known(b, 0, BATCHES):
                    evacuate(2)
                    evacuate(3)

            steps(sc_, step, STEPS_FROM, LOOP_FROM, LOOP_TO, STEPS_TO, 2)

            sc_.wait_ge(gate_done, BATCHES)
            act_(sig[:, :], logits[:, :], ACT.Sigmoid).then_inc(sig_done, 1)
            sc_.wait_ge(ffn_in, N_FFN)

            def shared(g, s, t):
                p = s % 2
                for c in range(CHUNKS):
                    wait(sc_, s_up_mm, 4 * g + c + 1)
                    if c == 0:
                        wait(sc_, s_down_mm, g - 1)
                    act_(s_act[p][:, c * SW:(c + 1) * SW], bank_s[:, c * 512:(c + 1) * 512], ACT.Gelu,
                         bias=s_upb[:, c:c + 1]).then_inc(s_gelu, 1)

            steps(sc_, shared, 0, 2, SGROUPS, SGROUPS, 2)

            def routed(j, s, t):
                p = s % 2
                wait(sc_, up_mm, j + 1)
                wait(sc_, down_mm, j - 1)
                for c in range(CHUNKS):
                    ins = act_(act[p][:, c * P:(c + 1) * P], bank_s[:, p * 512 + c * P:p * 512 + (c + 1) * P], ACT.Gelu,
                               bias=st_up[p][:, HIDDEN + c:HIDDEN + c + 1])
                ins.then_inc(gelu_done, 1)

            steps(sc_, routed, 0, 2, TILES, TILES, 2)

        @block.vector
        def _(dve):
            V = nc.vector
            own = [bass.AP(v[:, :].tensor, v[:, :].offset, [v[:, :].ap[0], [P + HD, HEADS], [1, HD]]) for v in val]
            dve.wait_ge(consts_in, N_CONSTS)
            dve.wait_ge(fills, 5)

            def step(i, s, t):
                b, p = i - 2, s % 2
                if known(b, 0, BATCHES):
                    wait(dve, recipt_mm, b + 1)
                    wait(dve, ot_done, b - 1)
                    V.tensor_copy(recipt[p][:, :], recipt_ps).then_inc(recipt_done, 1)
                    wait(dve, recipt_done, b + 1)
                    wait(dve, proj_mm, b - 1)
                wait(dve, stat2_done, min(i - 2, BATCHES) if isinstance(i, int) else i - 2)
                wait(dve, xn2_done, i - 4)
                if known(b, 0, BATCHES):
                    V.tensor_tensor(ot[p][:, :], ot_ps, recipt[p][:, :], ALU.mult).then_inc(ot_done, 1)
                if known(i - 3, 0, BATCHES):
                    p = (s - 3) % 2
                    V.bn_aggr(mv2[p][:, :], stat2[p][:, :]).then_inc(mv2_done, 1)
                b, p = i, s % 2
                if known(b, 0, BATCHES):
                    wait(dve, kvq_mm, b + 2)
                    wait(dve, pv_mm, 4 * (b - 1))
                    V.tensor_tensor(own[p],
                                    kv_v.rearrange("p (h d) -> p h d", d=HD),
                                    bv[:, :].rearrange("p (h d) -> p h d", d=HD), ALU.add).then_inc(v_done, 1)
                b, p = i + 1, (s + 1) % 2
                if known(b, 0, BATCHES):
                    wait(dve, kvq_mm, b + 1)
                    wait(dve, scores_mm, b - 1)
                    for dst, src, bias, mask, n, done in ((km, kv_k, bk, kmask, PER, km_done),
                                                          (qm, kv_q, bq, qmask, GROUPS, qm_done)):
                        if done is qm_done:
                            wait(dve, mv1_done, i + 2)
                        V.scalar_tensor_tensor(dst[p][:, :].rearrange("p (n k) -> p n k", k=P),
                                               src.unsqueeze(1).to_broadcast([P, n, P]), bias[:, 0:1],
                                               mask[:, :].unsqueeze(2).to_broadcast([P, n, P]),
                                               op0=ALU.add, op1=ALU.mult).then_inc(done, 1)
                b, p = i + 3, (s + 3) % 2
                if known(b, 0, BATCHES):
                    if isinstance(b, int):
                        dve.wait_ge(x_in[b * XCHUNKS // BATCHES], 16)
                        wait(dve, mv1_done, b - 1)
                    elif s == LOOP_FROM:
                        for c in range(1, XCHUNKS):
                            dve.wait_ge(x_in[c], 16)
                    V.bn_stats(stat1[p][:, :], tok(x, b)).then_inc(stat1_done, 1)
                    wait(dve, stat1_done, b + 1)
                    wait(dve, xn1_done, b - 1)
                b, p = i + 2, s % 2
                if known(b, 0, BATCHES):
                    wait(dve, rstd1_done, b + 1)
                    wait(dve, xn1t_mm, b - 1)
                    V.tensor_scalar(xn1[p][:, :], tok(x, b), mv1[p][:, 0:1], rstd1[p][:, 0:1],
                                    ALU.subtract, ALU.mult).then_inc(xn1_done, 1)
                if known(i + 3, 0, BATCHES):
                    p = (s + 3) % 2
                    V.bn_aggr(mv1[p][:, :], stat1[p][:, :]).then_inc(mv1_done, 1)
                b, p = i - 3, (s - 3) % 2
                if known(b, 0, BATCHES):
                    wait(dve, rstd2_done, b + 1)
                    wait(dve, xn2t_mm, b - 1)
                    wait(dve, xn2_kept, b - 1)
                    V.tensor_scalar(xn2s[p][:, :], tok(x, b), mv2[p][:, 0:1], rstd2[p][:, 0:1],
                                    ALU.subtract, ALU.mult).then_inc(xn2_done, 1)
                b, p = i, s % 2
                if known(b, 0, BATCHES):
                    wait(dve, scores_mm, b + 1)
                    wait(dve, max_done, b - 1)
                    wait(dve, exp_done, 4 * (b - 1))
                    V.tensor_scalar(clipped[p][:, :], bank_s[:, :], -CLAMP, CLAMP, ALU.max, ALU.min).then_inc(clip_done, 1)
                    wait(dve, clip_done, b + 1)
                    V.tensor_reduce(negmax[p][:, :], clipped[p][:, :].rearrange("p (h k) -> p h k", k=P), AX.X,
                                    ALU.max, negate=True).then_inc(max_done, 1)
                b, p = i - 1, (s - 1) % 2
                if known(b, 0, BATCHES):
                    wait(dve, exp_done, 4 * (b + 1))
                    wait(dve, recipt_mm, b - 1)
                    V.reciprocal(recip[p][:, :].rearrange("p (h d) -> p h d", d=HD),
                                 sums[p][:, :].unsqueeze(2).to_broadcast([P, HEADS, HD])).then_inc(recip_done, 1)
                b, p = i - 2, s % 2
                if known(b, 0, BATCHES):
                    wait(dve, proj_mm, b + 1)
                    if known(b - 1, 0, BATCHES):
                        wait(dve, gate_mm, b)
                    wait(dve, xb_done, b + 1)
                    V.tensor_tensor(tok(x, b), proj_ps, xb[p][:, :], ALU.add).then_inc(x1_done, 1)
                    wait(dve, x1_done, b + 1)
                    wait(dve, mv2_done, b - 1)
                b = i - 3
                if known(b, 0, BATCHES):
                    wait(dve, gate_mm, b + 1)
                    dst = logits[:, b * EXPERTS:(b + 1) * EXPERTS] if isinstance(b, int) else logits[:, bass.ds(b * EXPERTS, EXPERTS)]
                    V.tensor_tensor(dst, gate_ps, gate_b[:, :], ALU.add).then_inc(gate_done, 1)
                if known(i - 2, 0, BATCHES):
                    V.bn_stats(stat2[s % 2][:, :], tok(x, i - 2)).then_inc(stat2_done, 1)

            steps(dve, step, STEPS_FROM, LOOP_FROM, LOOP_TO, STEPS_TO, 2)

            count_of = [0]

            def do(ins):
                count_of[0] += 1
                ins.then_inc(route, 1)
                dve.wait_ge(route, count_of[0])

            def per_e(t):
                return t[:, :].unsqueeze(2).to_broadcast([P, BATCHES, EXPERTS])

            def per_t(t):
                return t[:, :].unsqueeze(1).to_broadcast([P, BATCHES, EXPERTS])

            dve.wait_ge(ffn_in, N_FFN)
            do(V.tensor_scalar(s_downb01[:, :], s_downb[:, :], 0.1, None, ALU.mult))
            dve.wait_ge(sig_done, 1)
            for k, scores in enumerate((sig, sig2)):
                do(V.tensor_reduce(best[k][:, :], by_e(scores), AX.X, ALU.max))
                do(V.tensor_tensor(by_e(eq), by_e(scores), per_e(best[k]), ALU.is_equal))
                do(V.tensor_tensor(by_e(sc), by_e(eq), per_t(rank_w), ALU.mult))
                do(V.tensor_reduce(win[:, :], by_e(sc), AX.X, ALU.max))
                do(V.tensor_tensor(by_e(oh[k]), by_e(sc), per_e(win), ALU.is_equal))
                if k == 0:
                    do(V.scalar_tensor_tensor(sig2[:, :], oh[0][:, :], -4.0, sig[:, :], op0=ALU.mult, op1=ALU.add))
            do(V.tensor_tensor(both[:, :], oh[0][:, :], oh[1][:, :], ALU.add))
            V.tensor_copy(eq[:, 0:1], both[:, 0:1]).then_inc(chosen, 1)
            dve.wait_ge(chosen, 1)
            do(V.scalar_tensor_tensor(den[:, :], best[0][:, :], 1e-6, best[1][:, :], op0=ALU.add, op1=ALU.add))
            do(V.reciprocal(rden[:, :], den[:, :]))
            for k in range(TOPK):
                do(V.tensor_tensor(weight[k][:, :], best[k][:, :], rden[:, :], ALU.mult))

            dve.wait_ge(rank_mm, 1)
            do(V.memset(pre_a[:, 0:EXPERTS], 0.0))
            do(V.tensor_copy(pre_a[:, EXPERTS:RE], bank_b[:, 0:RE - EXPERTS]))
            src, dst, d = pre_a, pre_b, EXPERTS
            while d < RE:
                do(V.tensor_copy(dst[:, 0:d], src[:, 0:d]))
                do(V.tensor_tensor(dst[:, d:RE], src[:, d:RE], src[:, 0:RE - d], ALU.add))
                src, dst, d = dst, src, 2 * d
            before = src
            do(V.tensor_tensor(count[:, :], before[:, RE - EXPERTS:RE], bank_b[:, RE - EXPERTS:RE], ALU.add))
            do(V.tensor_scalar(count_i[:, :], count[:, :], float(P - 1), None, ALU.add))
            do(V.tensor_scalar(count_j[:, :], count_i[:, :], 7, 7, ALU.logical_shift_right, ALU.logical_shift_left))
            do(V.tensor_copy(padded[:, :], count_j[:, :]))
            do(V.tensor_copy(base_a[:, :], padded[:, :]))
            src, dst, d = base_a, base_b, 1
            while d < EXPERTS:
                do(V.tensor_copy(dst[:, 0:d], src[:, 0:d]))
                do(V.tensor_tensor(dst[:, d:EXPERTS], src[:, d:EXPERTS], src[:, 0:EXPERTS - d], ALU.add))
                src, dst, d = dst, src, 2 * d
            do(V.tensor_copy(ends[:, :], src[:, :]))
            do(V.tensor_tensor(dst[:, :], ends[:, :], padded[:, :], ALU.subtract))
            starts = dst
            do(V.tensor_tensor(slot_of[:, :], before[:, :], bank_a[:, 0:RE], ALU.add))
            do(V.tensor_tensor(by_e(sig2), by_e(slot_of), per_t(starts), ALU.add))
            for k in range(TOPK):
                do(V.tensor_tensor(sc[:, :], sig2[:, :], oh[k][:, :], ALU.mult))
                do(V.tensor_reduce(slot_f[k][:, :], by_e(sc), AX.X, ALU.add))
                do(V.tensor_copy(slot[k][:, :], slot_f[k][:, :]))
            V.tensor_copy(eq[:, 1:2], ends[:, 0:1]).then_inc(slots_done, 1)
            do(V.tensor_tensor(passed[:, :].rearrange("p (j e) -> p j e", e=EXPERTS),
                               ends[:, :].unsqueeze(1).to_broadcast([P, TILES, EXPERTS]),
                               tile_at[:, :].unsqueeze(2).to_broadcast([P, TILES, EXPERTS]), ALU.is_le))
            do(V.tensor_reduce(expert_f[:, :], passed[:, :].rearrange("p (j e) -> p j e", e=EXPERTS), AX.X, ALU.add))
            do(V.tensor_scalar(expert_g[:, :], expert_f[:, :], float(EXPERTS - 1), None, ALU.min))
            do(V.tensor_copy(expert[:, :], expert_g[:, :]))

            def shared(g, s, t):
                p = s % 2
                xg = tok(x, g * SG, SG)
                V.tensor_tensor(xg.rearrange("p (b c) -> p b c", c=P), xg.rearrange("p (b c) -> p b c", c=P),
                                s_downb01[:, :].unsqueeze(1).to_broadcast([P, SG, P]), ALU.add).then_inc(s_bias, 1)
                wait(dve, s_bias, g + 1)
                wait(dve, s_down_mm, g + 1)
                V.scalar_tensor_tensor(xg, bank_t[p][:, :], 0.1, xg, op0=ALU.mult, op1=ALU.add).then_inc(s_added, 1)

            steps(dve, shared, 0, 2, SGROUPS, SGROUPS, 2)

            def routed(j, s, t):
                def expert_of(b):
                    at = expert[0:1, b:b + 1] if isinstance(b, int) else expert[0:1, bass.ds(b, 1)]
                    return V.value_load(at, min_val=0, max_val=EXPERTS - 1)

                if known(j + 1, 0, TILES):
                    next_expert = expert_of(j + 1)
                if known(j, 0, TILES):
                    this_expert = expert_of(j)
                b, p = j - 2, s % 2
                if known(b, 0, TILES):
                    wait(dve, down_mm, b + 1)
                    if b + 1 > RING if isinstance(b, int) else True:
                        n = (s - 2) % RING
                        dve.wait_ge(y_out[n], (t + (s - 2) // RING) * 16)
                    V.tensor_tensor(y[(s - 2) % RING][:, :], bank_t[p][:, 0:P], st_down[p][:, HIDDEN:DNW],
                                    ALU.add).then_inc(y_done, 1)
                b, p = j + 1, (s + 1) % 2
                if known(b, 0, TILES):
                    wait(dve, xst_mm, b + 1)
                    wait(dve, up_mm, b - 1)
                    V.tensor_copy(xst[p][:, :], (bank_a, bank_b)[p][:, 0:P]).then_inc(xst_done, 1)
                    wait(dve, gelu_done, b - 1)
                    V.tensor_copy(st_up[p][:, :], up_w[:, bass.ds(next_expert * UPW, UPW)]).then_inc(up_w_done, 1)
                b, p = j, s % 2
                if known(b, 0, TILES):
                    wait(dve, down_mm, b - 1)
                    wait(dve, y_done, b - 1)
                    V.tensor_copy(st_down[p][:, :], down_w[:, bass.ds(this_expert * DNW, DNW)]).then_inc(down_w_done, 1)

            steps(dve, routed, -1, 7, TILES - 1, TILES + 2, RING)

            for t in range(BATCHES):
                n, p = t % RING, t % 2
                dve.wait_ge(y_in[n], 16 * TOPK * (t // RING + 1))
                if t >= 2:
                    dve.wait_ge(summed, t - 1)
                V.scalar_tensor_tensor(part[p][:, :], yg[n][:, 0:P], weight[0][:, t:t + 1], tok(x, t),
                                       op0=ALU.mult, op1=ALU.add).then_inc(half_sum, 1)
                dve.wait_ge(half_sum, t + 1)
                V.scalar_tensor_tensor(tok(x, t), yg[n][:, P:2 * P], weight[1][:, t:t + 1], part[p][:, :],
                                       op0=ALU.mult, op1=ALU.add).then_inc(summed, 1)


def kernel(x, ctx_768, L0_xattn_Wq, L0_xattn_bq, L0_xattn_Wk, L0_xattn_bk, L0_xattn_Wv, L0_xattn_bv,
           L0_xattn_Wo, L0_xattn_bo, L0_ffn_gate_w, L0_ffn_gate_bias, L0_ffn_Wu, L0_ffn_bu, L0_ffn_Wd,
           L0_ffn_bd, L0_ffn_sWu, L0_ffn_sbu, L0_ffn_sWd, L0_ffn_sbd):
    import concourse.bacc as bacc
    import numpy as np
    from concourse.bass_utils import run_bass_kernel_spmd

    def rows_of(w):
        w = np.asarray(w)
        w = w.reshape(w.shape[:-1] + (CHUNKS, P))
        order = (w.ndim - 1,) + tuple(range(w.ndim - 3)) + (w.ndim - 2, w.ndim - 3)
        return w.transpose(order)

    part = np.arange(P)
    data = {
        "x": x,
        "ctxt": np.asarray(ctx_768).transpose(2, 0, 1).reshape(CTX, TOKENS),
        "wq": L0_xattn_Wq, "wk": L0_xattn_Wk, "wv": L0_xattn_Wv, "wo": L0_xattn_Wo,
        "bq": np.asarray(L0_xattn_bq).reshape(P, 1), "bk": np.asarray(L0_xattn_bk).reshape(P, 1),
        "bv": L0_xattn_bv, "bo": L0_xattn_bo,
        "gate_w": np.asarray(L0_ffn_gate_w).transpose(1, 0), "gate_b": L0_ffn_gate_bias,
        "up": np.asarray(L0_ffn_Wu).transpose(2, 0, 1),
        "upb": np.asarray(L0_ffn_bu).reshape(EXPERTS, CHUNKS, P).transpose(2, 0, 1),
        "down": rows_of(L0_ffn_Wd).reshape(P, EXPERTS, HIDDEN),
        "downb": L0_ffn_bd,
        "s_up": np.asarray(L0_ffn_sWu).transpose(1, 0),
        "s_upb": np.asarray(L0_ffn_sbu).reshape(CHUNKS, P).transpose(1, 0),
        "s_down": rows_of(L0_ffn_sWd).reshape(P, HIDDEN),
        "s_downb": L0_ffn_sbd,
        "ident": np.eye(P, dtype=np.float32),
        "tri": np.triu(np.ones((P, P), np.float32), 1),
        "qmask": (part[:, None] // (P // GROUPS) == np.arange(GROUPS)).astype(np.float32) * np.float32(HD ** -0.5),
        "kmask": (part[:, None] // HD % PER == np.arange(PER)).astype(np.float32),
        "rank_w": np.arange(EXPERTS, 0, -1, dtype=np.float32),
        "tile_at": np.arange(TILES, dtype=np.float32) * np.float32(P),
    }
    nc = bacc.Bacc("TRN2", target_bir_lowering=False, num_devices=1)
    arrays, dr = {}, {}
    for name, a in data.items():
        arrays[f"in_{name}"] = np.ascontiguousarray(a)
        dr[name] = nc.dram_tensor(f"in_{name}", arrays[f"in_{name}"].shape, F32, kind="ExternalInput").ap()
    out = nc.dram_tensor("out_dram", (BATCHES, P, P), F32, kind="ExternalOutput").ap()
    xattn_moe(nc, dr, out)
    return run_bass_kernel_spmd(nc, [arrays], core_ids=[0]).results[0]["out_dram"]
```

```python
from contextlib import ExitStack

import concourse.bass as bass
from concourse import mybir

F32 = mybir.dt.float32
I32 = mybir.dt.int32
U32 = mybir.dt.uint32
ALU = mybir.AluOpType
ACT = mybir.ActivationFunctionType
AX = mybir.AxisListType

P = 128
BATCHES = 32
CTX = 96
HEADS = 16
HD = P // HEADS
GROUPS = 4
PER = HEADS // GROUPS
CLAMP = 10000.0
EPS = 1e-5
TOKENS = BATCHES * P
EXPERTS = 8
TOPK = 2
CHUNKS = 4
HIDDEN = CHUNKS * P
PARTS = 2
PART = (0, 20, BATCHES)
PTILE = (0, TOPK * PART[1] + EXPERTS - 1, TOPK * PART[2] + 2 * (EXPERTS - 1))
TILES = PTILE[PARTS]
UPW = HIDDEN + CHUNKS
DNW = HIDDEN + P
SG = 4
SGROUPS = BATCHES // SG
SW = SG * P
RING = 4
STORE_LAG = 7
TURN = 8
YGROUP = 2
XCHUNKS = 4
EARLY = 6
LOOP_FROM, LOOP_TO = 6, 28
COLS = (("wq", P), ("wk", P), ("wv", P), ("wo", P), ("gate_w", EXPERTS), ("ident", P), ("tri", P),
        ("qmask", GROUPS), ("kmask", PER), ("bq", 1), ("bk", 1))
ROWS = (("bv", P), ("bo", P), ("gate_b", EXPERTS), ("rank_w", EXPERTS), ("tile_at", TILES))
STEPS_FROM, STEPS_TO = -3, BATCHES + 3


def wait(eng, sem, count):
    if not isinstance(count, int) or count > 0:
        eng.wait_ge(sem, count)


def known(i, lo, hi):
    return not isinstance(i, int) or lo <= i < hi


def steps(eng, body, first, loop_from, loop_to, last, unroll):
    for i in range(first, loop_from):
        body(i, i, 0)
    with eng.Fori(0, (loop_to - loop_from) // unroll) as t:
        for u in range(unroll):
            body(t * unroll + (loop_from + u), loop_from + u, t)
    for i in range(loop_to, last):
        body(i, i, 0)


def use_of(s, t):
    return t * (TURN // RING) + s // RING


def loop_end(start, end, unroll):
    return start + (end - start) // unroll * unroll


def xattn_moe(nc, dr, out):
    ctx_stack = ExitStack()
    with ctx_stack:
        def sb(name, shape, dt=F32):
            return ctx_stack.enter_context(nc.sbuf_tensor(name, shape, dt))

        def psum(name, width):
            return ctx_stack.enter_context(nc.psum_tensor(name, [P, width], F32))

        def sem(name):
            return ctx_stack.enter_context(nc.semaphore(name))

        cols, rows = sb("cols", [P, sum(w for _, w in COLS)]), sb("rows", [P, sum(w for _, w in ROWS)])

        def piece(t, parts, name):
            names = [n for n, _ in parts]
            at = sum(w for _, w in parts[:names.index(name)])
            return t[:, at:at + parts[names.index(name)][1]]

        wq, wk, wv, wo, gate_w, ident, tri, qmask, kmask, bq, bk = (piece(cols, COLS, n) for n, _ in COLS)
        wk, wv = wk[0:CTX, :], wv[0:CTX, :]
        bv, bo, gate_b, rank_w, tile_at = (piece(rows, ROWS, n) for n, _ in ROWS)
        ones = sb("ones", [P, P])
        up_w = sb("up_w", [P, EXPERTS * UPW])
        down_w = sb("down_w", [P, EXPERTS * DNW])
        s_up, s_upb, s_down = sb("s_up", [P, HIDDEN]), sb("s_upb", [P, CHUNKS]), sb("s_down", [P, HIDDEN])
        s_downb, s_downb01 = sb("s_downb", [P, P]), sb("s_downb01", [P, P])
        minus_half, eps = sb("minus_half", [P, 1]), sb("eps", [P, 1])
        zero = sb("zero", [P, P])

        x = sb("x", [P, TOKENS])
        xn2 = sb("xn2", [P, TOKENS])
        xn2t = sb("xn2t", [P, TOKENS])
        logits = sb("logits", [P, BATCHES * EXPERTS])

        def two(name, shape, dt=F32):
            return [sb(f"{name}{n}", shape, dt) for n in range(2)]

        ctxt = two("ctxt", [CTX, P])
        xn1, xn1t = two("xn1", [P, P]), two("xn1t", [P, P])
        stat1, mv1, ve1, rstd1 = two("stat1_", [P, 6]), two("mv1_", [P, 2]), two("ve1_", [P, 1]), two("rstd1_", [P, 1])
        stat2, mv2, ve2, rstd2 = two("stat2_", [P, 6]), two("mv2_", [P, 2]), two("ve2_", [P, 1]), two("rstd2_", [P, 1])
        km, qm = two("km", [P, PER * P]), two("qm", [P, GROUPS * P])
        val = two("val", [P, HEADS * P])
        clipped, probs = two("clipped", [P, HEADS * P]), two("probs", [P, HEADS * P])
        negmax, sums, rsum = two("negmax", [P, HEADS]), two("sums", [P, HEADS]), two("rsum", [P, HEADS])
        recip, recipt = two("recip", [P, P]), two("recipt", [P, P])
        probst = two("probst", [P, PER * P])
        ot, xb = two("ot", [P, P]), two("xb", [P, P])
        xn2s, xn2ts = two("xn2s", [P, P]), two("xn2ts", [P, P])

        bank_s = psum("bank_s", GROUPS * 512)
        bank_t = [psum(f"bank_t{n}", 512) for n in range(2)]
        bank_a, bank_b = psum("bank_a", 512), psum("bank_b", 512)
        kv_k, kv_v, kv_q = bank_a[:, 0:P], bank_a[:, P:2 * P], bank_a[:, 2 * P:3 * P]
        proj_ps, gate_ps = bank_a[:, 0:P], bank_a[:, P:P + EXPERTS]
        xn1t_ps, xn2t_ps = bank_a[:, 0:P], bank_a[:, P:2 * P]
        ot_ps, recipt_ps = bank_b[:, 0:P], bank_b[:, P:2 * P]

        consts_in = sem("consts_in")
        ffn_in = sem("ffn_in")
        x_in = [sem(f"x_in{n}") for n in range(XCHUNKS)]
        ctx_in = [sem(f"ctx_in{n}") for n in range(2)]
        fills = sem("fills")
        zeroed = sem("zeroed")
        slots_zeroed = sem("slots_zeroed")
        stat1_done, mv1_done, ve1_done, rstd1_done = sem("stat1_done"), sem("mv1_done"), sem("ve1_done"), sem("rstd1_done")
        stat2_done, mv2_done, ve2_done, rstd2_done = sem("stat2_done"), sem("mv2_done"), sem("ve2_done"), sem("rstd2_done")
        xn1_done, xn1t_mm, xn1t_done = sem("xn1_done"), sem("xn1t_mm"), sem("xn1t_done")
        kvq_mm, v_done, km_done, qm_done = sem("kvq_mm"), sem("v_done"), sem("km_done"), sem("qm_done")
        scores_mm, clip_done, max_done = sem("scores_mm"), sem("clip_done"), sem("max_done")
        exp_done = sem("exp_done")
        probst_mm, probst_done, pv_mm = sem("probst_mm"), sem("probst_done"), sem("pv_mm")
        rsum_done = sem("rsum_done")
        recip_done, recipt_mm, recipt_done, ot_done = sem("recip_done"), sem("recipt_mm"), sem("recipt_done"), sem("ot_done")
        proj_mm, xb_done, x1_done = sem("proj_mm"), sem("xb_done"), sem("x1_done")
        xn2_done, xn2t_mm, xn2t_done = sem("xn2_done"), sem("xn2t_mm"), sem("xn2t_done")
        gate_mm, gate_done = sem("gate_mm"), sem("gate_done")
        xn2_kept, xn2t_kept = sem("xn2_kept"), sem("xn2t_kept")

        sig_done, route = sem("sig_done"), sem("route")
        chosen, rank_mm, slots_done = sem("chosen"), sem("rank_mm"), sem("slots_done")
        scattered = [sem(f"scattered{p}") for p in range(PARTS)]
        s_up_mm, s_gelu = sem("s_up_mm"), sem("s_gelu")
        s_down_mm, s_bias, s_added = sem("s_down_mm"), sem("s_bias"), sem("s_added")
        xs_in = [sem(f"xs_in{n}") for n in range(RING)]
        xst_mm, xst_done, up_w_done, down_w_done = sem("xst_mm"), sem("xst_done"), sem("up_w_done"), sem("down_w_done")
        up_mm, gelu_done, down_mm, y_done = sem("up_mm"), sem("gelu_done"), sem("down_mm"), sem("y_done")
        y_out = [sem(f"y_out{n}") for n in range(RING)]
        y_in = [sem(f"y_in{n}") for n in range(BATCHES // YGROUP)]
        half_sum, summed = sem("half_sum"), sem("summed")
        stored = sem("stored")

        RE = BATCHES * EXPERTS
        sig, sig2, eq, sc = (sb(n, [P, RE]) for n in ("sig", "sig2", "eq", "sc"))
        oh = [sb(f"oh{k}", [P, RE]) for k in range(TOPK)]
        both, pre_a, pre_b, slot_of = (sb(n, [P, RE]) for n in ("both", "pre_a", "pre_b", "slot_of"))
        best = [sb(f"best{k}", [P, BATCHES]) for k in range(TOPK)]
        win, den, rden = (sb(n, [P, BATCHES]) for n in ("win", "den", "rden"))
        weight = [sb(f"weight{k}", [P, BATCHES]) for k in range(TOPK)]
        slot_f = [sb(f"slot_f{k}", [P, BATCHES]) for k in range(TOPK)]
        slot = [sb(f"slot{k}", [P, BATCHES], I32) for k in range(TOPK)]
        SETS = PARTS * EXPERTS
        count, padded, base_a, base_b, ends, starts = (
            sb(n, [P, SETS]) for n in ("count", "padded", "base_a", "base_b", "ends", "starts"))
        count_i, count_j = sb("count_i", [P, SETS], I32), sb("count_j", [P, SETS], I32)
        passed = sb("passed", [P, TILES * EXPERTS])
        expert_f, expert_g = sb("expert_f", [P, TILES]), sb("expert_g", [P, TILES])
        expert = sb("expert", [P, TILES], I32)
        s_act = probs
        xs = [sb(f"xs{n}", [P, P]) for n in range(RING)]
        xst = two("xst", [P, P])
        st_up = two("st_up", [P, UPW])
        st_down = [clipped[n // 2][:, n % 2 * DNW:(n % 2 + 1) * DNW] for n in range(RING)]
        act = two("act", [P, HIDDEN])
        y = [sb(f"y{n}", [P, P]) for n in range(RING)]
        yg = (xn2, xn2t)
        part = two("part", [P, P])

        slots_x, slots_y = ([nc.dram_tensor(f"{name}{p}", ((PTILE[p + 1] - PTILE[p]) * P, P), F32).ap()
                             for p in range(PARTS)] for name in ("slots_x", "slots_y"))

        def tok(t, b, n=1):
            return t[:, bass.ds(b * P, n * P)] if not isinstance(b, int) else t[:, b * P:(b + n) * P]

        def by_e(t):
            return t[:, :].rearrange("p (t e) -> p t e", e=EXPERTS)

        N_CONSTS = 16 * 2
        N_FFN = 16 * (5 + 2 * EXPERTS)

        block = ctx_stack.enter_context(nc.Block())

        @block.sync
        def _(sp):
            xv = dr["x"].rearrange("b s c -> s b c")
            n = BATCHES // XCHUNKS

            def load_x(c):
                sp.dma_start(tok(x, c * n, n).rearrange("p (b c) -> p b c", c=P),
                             xv[:, c * n:(c + 1) * n, :]).then_inc(x_in[c], 16)

            def load_ctx(b, s, t):
                wait(sp, kvq_mm, b)
                src = dr["ctxt"][:, b * P:(b + 1) * P] if isinstance(b, int) else dr["ctxt"][:, bass.ds(b * P, P)]
                sp.dma_start(ctxt[s % 2][:, :], src).then_inc(ctx_in[s % 2], 16)

            sp.dma_start(cols[:, :], dr["cols"]).then_inc(consts_in, 16)
            load_x(0)
            sp.dma_start(rows[:, :], dr["rows"].partition_broadcast(P)).then_inc(consts_in, 16)
            load_ctx(0, 0, 0)
            load_ctx(1, 1, 0)
            for c in range(1, XCHUNKS):
                load_x(c)
            for e in range(EXPERTS):
                with sp.Fori(2 * e + 1, min(2 * e + 3, BATCHES // 2)) as t:
                    load_ctx(t * 2, 0, t)
                    load_ctx(t * 2 + 1, 1, t)
                sp.dma_start(up_w[:, e * UPW:(e + 1) * UPW], dr["up"][:, e * UPW:(e + 1) * UPW]).then_inc(ffn_in, 16)
                sp.dma_start(down_w[:, e * DNW:e * DNW + HIDDEN],
                             dr["down"][:, e * HIDDEN:(e + 1) * HIDDEN]).then_inc(ffn_in, 16)
                sp.wait_ge(zeroed, 1)
                n = EXPERTS // PARTS
                p, piece_ = e // n, e % n
                tiles = PTILE[p + 1] - PTILE[p]
                lo, hi = piece_ * tiles // n, (piece_ + 1) * tiles // n
                sp.dma_start(slots_x[p][lo * P:hi * P, :].rearrange("(t p) c -> p t c", p=P),
                             zero[:, :].unsqueeze(1).to_broadcast([P, hi - lo, P])).then_inc(slots_zeroed, 16)
            dnv = down_w[:, :].rearrange("p (e w) -> p e w", w=DNW)
            sp.dma_start(dnv[:, :, HIDDEN:DNW], dr["downb"].partition_broadcast(P)).then_inc(ffn_in, 16)
            sp.dma_start(s_up[:, :], dr["s_up"]).then_inc(ffn_in, 16)
            sp.dma_start(s_down[:, :], dr["s_down"]).then_inc(ffn_in, 16)
            sp.dma_start(s_upb[:, :], dr["s_upb"]).then_inc(ffn_in, 16)
            sp.dma_start(s_downb[:, :], dr["s_downb"].partition_broadcast(P)).then_inc(ffn_in, 16)

            def slot_rows(parts, j, s):
                p = int(s >= PTILE[1])
                j = j - PTILE[p]
                return parts[p][j * P:(j + 1) * P, :] if isinstance(j, int) else parts[p][bass.ds(j * P, P), :]

            def tile_io(j, s, t):
                if known(j, 0, TILES):
                    wait(sp, xst_mm, j - RING + 1)
                    sp.dma_start(xs[s % RING][:, :], slot_rows(slots_x, j, s)).then_inc(xs_in[s % RING], 16)
                b, n = j - STORE_LAG, (s - STORE_LAG) % RING
                if known(b, 0, TILES):
                    wait(sp, y_done, b + 1)
                    sp.dma_start(slot_rows(slots_y, b, s - STORE_LAG), y[n][:, :]).then_inc(y_out[n], 16)

            sp.wait_ge(scattered[0], 16 * TOPK * PART[1])
            steps(sp, tile_io, 0, STORE_LAG, loop_end(STORE_LAG, PTILE[1], RING), PTILE[1], RING)
            sp.wait_ge(scattered[1], 16 * TOPK * (BATCHES - PART[1]))
            start = PTILE[1] + STORE_LAG
            steps(sp, tile_io, PTILE[1], start, loop_end(start, TILES, RING), TILES + STORE_LAG, RING)

            ov = out.rearrange("b s c -> s b c")
            for g in range(SGROUPS):
                sp.wait_ge(summed, (g + 1) * SG)
                sp.dma_start(ov[:, g * SG:(g + 1) * SG, :],
                             tok(x, g * SG, SG).rearrange("p (b c) -> p b c", c=P)).then_inc(stored, 16)
            sp.wait_ge(stored, 16 * SGROUPS)

        @block.gpsimd
        def _(pool):
            nc.gpsimd.memset(minus_half[:, :], -0.5).then_inc(fills, 1)
            nc.gpsimd.memset(eps[:, :], EPS).then_inc(fills, 1)
            nc.gpsimd.memset(zero[:, :], 0.0).then_inc(zeroed, 1)
            nc.gpsimd.memset(ones[:, :], 1.0).then_inc(fills, 1)
            for v in val:
                nc.gpsimd.memset(v[:, :], 0.0).then_inc(fills, 1)
            pool.wait_ge(fills, 5)
            pool.wait_ge(consts_in, N_CONSTS)

            def rstd(b, mv, ve, out_, mv_done, ve_done, done, used, s):
                wait(pool, mv_done, b + 1)
                wait(pool, used, b - 1)
                nc.gpsimd.tensor_tensor(ve[s][:, :], mv[s][:, 1:2], eps[:, :], ALU.add).then_inc(ve_done, 1)
                wait(pool, ve_done, b + 1)
                nc.gpsimd.tensor_tensor(out_[s][:, :], ve[s][:, :], minus_half[:, :], ALU.pow).then_inc(done, 1)

            def step(i, s, t):
                if known(i - 3, 0, BATCHES):
                    rstd(i - 3, mv2, ve2, rstd2, mv2_done, ve2_done, rstd2_done, xn2_done, (s - 3) % 2)
                if known(i + 3, 0, BATCHES):
                    rstd(i + 3, mv1, ve1, rstd1, mv1_done, ve1_done, rstd1_done, xn1_done, (s + 3) % 2)
                b = i - 1
                if known(b, 0, BATCHES):
                    wait(pool, x1_done, b - 1)
                    nc.gpsimd.tensor_tensor(xb[(s - 1) % 2][:, :], tok(x, b), bo[:, :], ALU.add).then_inc(xb_done, 1)
                b, p = i - 3, (s - 3) % 2
                if known(b, 0, BATCHES):
                    wait(pool, xn2_done, b + 1)
                    nc.gpsimd.tensor_copy(tok(xn2, b), xn2s[p][:, :]).then_inc(xn2_kept, 1)
                    wait(pool, xn2t_done, b + 1)
                    nc.gpsimd.tensor_copy(tok(xn2t, b), xn2ts[p][:, :]).then_inc(xn2t_kept, 1)

            steps(pool, step, STEPS_FROM, LOOP_FROM, LOOP_TO, STEPS_TO, 2)

            pool.wait_ge(slots_zeroed, 16 * EXPERTS)
            pool.wait_ge(xn2_kept, BATCHES)
            pool.wait_ge(slots_done, 1)
            for t in range(BATCHES):
                for k in range(TOPK):
                    nc.gpsimd.indirect_dma_start(
                        out=slots_x[t >= PART[1]], out_offset=bass.IndirectOffsetOnAxis(ap=slot[k][:, t:t + 1].bitcast(U32), axis=0),
                        in_=tok(xn2, t), in_offset=None).then_inc(scattered[t >= PART[1]], 16)
            for p in range(PARTS):
                pool.wait_ge(scattered[p], 16 * TOPK * (PART[p + 1] - PART[p]))
            pool.wait_ge(s_up_mm, 4 * SGROUPS)
            for p in range(PARTS):
                for n in range(RING):
                    pool.wait_ge(y_out[n], 16 * len(range(n, PTILE[p + 1], RING)))
                for t in range(PART[p], PART[p + 1]):
                    for k in range(TOPK):
                        nc.gpsimd.indirect_dma_start(
                            out=tok(yg[k], t), out_offset=None, in_=slots_y[p],
                            in_offset=bass.IndirectOffsetOnAxis(ap=slot[k][:, t:t + 1].bitcast(U32), axis=0),
                        ).then_inc(y_in[t // YGROUP], 16)

        @block.tensor
        def _(pe):
            mm, tr = nc.tensor.matmul, nc.tensor.transpose
            pe.wait_ge(consts_in, N_CONSTS)
            pe.wait_ge(fills, 5)

            def step(i, s, t):
                b, p = i + 1, (s + 1) % 2
                if known(b, 0, BATCHES) or known(i, 0, BATCHES):
                    wait(pe, qm_done, min(b, BATCHES) if isinstance(b, int) else b)
                    wait(pe, v_done, i)
                    wait(pe, x1_done, b - 3)
                    wait(pe, gate_done, b - 4)
                    wait(pe, xn1t_done, min(b + 1, BATCHES) if isinstance(b, int) else b + 1)
                if known(i, 0, BATCHES):
                    last = mm(kv_v, ctxt[s % 2][:, :], wv[:, :], start=True, stop=True)
                if known(b, 0, BATCHES):
                    pe.wait_ge(ctx_in[p], (t + (s + 1) // 2 + 1) * 16)
                    mm(kv_k, wk[:, :], ctxt[p][:, :], start=True, stop=True)
                    last = mm(kv_q, wq[:, :], xn1t[p][:, :], start=True, stop=True)
                if known(b, 0, BATCHES) or known(i, 0, BATCHES):
                    last.then_inc(kvq_mm, 1)
                b, p = i, s % 2
                if known(b, 0, BATCHES):
                    wait(pe, qm_done, b + 1)
                    for half in range(2):
                        wait(pe, clip_done, 2 * (b - 1) + half + 1)
                        for j in range(half * GROUPS // 2, (half + 1) * GROUPS // 2):
                            last = mm(bank_s[:, j * 512:(j + 1) * 512], qm[p][:, j * P:(j + 1) * P], km[p][:, :],
                                      start=True, stop=True)
                        last.then_inc(scores_mm, 1)
                b, p = i - 1, (s - 1) % 2

                def turn(g):
                    wait(pe, exp_done, 4 * b + g + 1)
                    wait(pe, probst_done, 4 * b + g - 1)
                    for r in range(PER):
                        h = g * PER + r
                        last = tr(bank_t[g % 2][:, r * P:(r + 1) * P], probs[p][:, h * P:(h + 1) * P], ident[:, :])
                    last.then_inc(probst_mm, 1)

                def weigh(g):
                    wait(pe, probst_done, 4 * b + g + 1)
                    if g == 0:
                        wait(pe, v_done, b + 1)
                        wait(pe, ot_done, b)
                    for r in range(PER):
                        h = g * PER + r
                        last = mm(ot_ps, val[p][:, h * P:(h + 1) * P], probst[g % 2][:, r * P:(r + 1) * P],
                                  start=(h == 0), stop=(h == HEADS - 1))
                    last.then_inc(pv_mm, 1)

                if known(b, 0, BATCHES):
                    turn(0)
                    turn(1)
                if known(i + 2, 0, BATCHES) or known(i - 3, 0, BATCHES):
                    wait(pe, v_done, min(i + 1, BATCHES) if isinstance(i, int) else i + 1)
                    wait(pe, qm_done, min(i + 2, BATCHES) if isinstance(i, int) else i + 2)
                    if isinstance(i, int) and i >= BATCHES:
                        wait(pe, x1_done, i - 2)
                        wait(pe, gate_done, i - 3)
                if known(i - 3, 0, BATCHES):
                    wait(pe, xn2_done, i - 2)
                    tr(xn2t_ps, xn2s[(s - 3) % 2][:, :], ident[:, :]).then_inc(xn2t_mm, 1)
                if known(i + 2, 0, BATCHES):
                    wait(pe, xn1_done, i + 3)
                    tr(xn1t_ps, xn1[s % 2][:, :], ident[:, :]).then_inc(xn1t_mm, 1)
                if known(b, 0, BATCHES):
                    weigh(0)
                    turn(2)
                if known(i - 2, 0, BATCHES) or known(i - 3, 0, BATCHES):
                    wait(pe, xn1t_done, min(i + 3, BATCHES) if isinstance(i, int) else i + 3)
                    wait(pe, xn2t_done, i - 2)
                if known(i - 2, 0, BATCHES):
                    wait(pe, ot_done, i - 1)
                    mm(proj_ps, ot[s % 2][:, :], wo[:, :], start=True, stop=True).then_inc(proj_mm, 1)
                if known(i - 3, 0, BATCHES):
                    mm(gate_ps, xn2ts[(s - 3) % 2][:, :], gate_w[:, :], start=True, stop=True).then_inc(gate_mm, 1)
                if known(b, 0, BATCHES):
                    weigh(1)
                    turn(3)
                    weigh(2)
                    weigh(3)
                    wait(pe, recip_done, b + 1)
                    tr(recipt_ps, recip[p][:, :], ident[:, :]).then_inc(recipt_mm, 1)

            steps(pe, step, STEPS_FROM, LOOP_FROM, LOOP_TO, STEPS_TO, 2)

            pe.wait_ge(ffn_in, N_FFN)
            pe.wait_ge(clip_done, 2 * BATCHES)
            pe.wait_ge(xn2t_kept, BATCHES)
            pe.wait_ge(probst_done, 4 * BATCHES)
            pe.wait_ge(ot_done, BATCHES)

            def shared(g, s, t):
                if known(g, 0, SGROUPS):
                    for c in range(CHUNKS):
                        wait(pe, s_gelu, 4 * (g - 1) + c + 1)
                        mm(bank_s[:, c * 512:(c + 1) * 512], s_up[:, c * P:(c + 1) * P],
                           tok(xn2t, g * SG, SG), start=True, stop=True).then_inc(s_up_mm, 1)
                b, p = g - 1, (s - 1) % 2
                if known(b, 0, SGROUPS):
                    wait(pe, s_gelu, 4 * (b + 1))
                    wait(pe, s_added, b - 1)
                    for q in range(SG):
                        for c in range(CHUNKS):
                            last = mm(bank_t[p][:, q * P:(q + 1) * P], s_act[p][:, c * SW + q * P:c * SW + (q + 1) * P],
                                      s_down[:, c * P:(c + 1) * P], start=(c == 0), stop=(c == CHUNKS - 1))
                    last.then_inc(s_down_mm, 1)

            shared(0, 0, 0)
            pe.wait_ge(chosen, 1)
            pe.wait_ge(gate_done, BATCHES)
            mm(bank_a[:, 0:RE], tri[:, :], both[:, :], start=True, stop=True)
            mm(bank_b[:, 0:RE], ones[:, :], both[:, :], start=True, stop=True).then_inc(rank_mm, 1)
            steps(pe, shared, 1, 2, SGROUPS, SGROUPS + 1, 2)

            pe.wait_ge(slots_done, 1)
            pe.wait_ge(s_gelu, 4 * SGROUPS)
            pe.wait_ge(s_added, SGROUPS)

            def routed(j, s, t):
                b, p = j + 1, (s + 1) % 2
                if known(b, 0, TILES):
                    pe.wait_ge(xs_in[(s + 1) % RING], (use_of(s + 1, t) + 1) * 16)
                    wait(pe, xst_done, b - 1)
                    tr((bank_a, bank_b)[p][:, 0:P], xs[(s + 1) % RING][:, :], ident[:, :]).then_inc(xst_mm, 1)
                b, p = j, s % 2
                if known(b, 0, TILES):
                    wait(pe, xst_done, b + 1)
                    wait(pe, up_w_done, b + 1)
                    wait(pe, gelu_done, b - 1)
                    for c in range(CHUNKS):
                        last = mm(bank_s[:, p * 512 + c * P:p * 512 + (c + 1) * P], st_up[p][:, c * P:(c + 1) * P],
                                  xst[p][:, :], start=True, stop=True)
                    last.then_inc(up_mm, 1)
                b, p = j - 1, (s - 1) % 2
                if known(b, 0, TILES):
                    wait(pe, gelu_done, b + 1)
                    wait(pe, down_w_done, b + 1)
                    wait(pe, y_done, b - 1)
                    w = st_down[(s - 1) % RING]
                    for c in range(CHUNKS):
                        last = mm(bank_t[p][:, 0:P], act[p][:, c * P:(c + 1) * P], w[:, c * P:(c + 1) * P],
                                  start=(c == 0), stop=(c == CHUNKS - 1))
                    last.then_inc(down_mm, 1)

            steps(pe, routed, -1, 3, loop_end(3, TILES - 1, TURN), TILES + 1, TURN)

        @block.scalar
        def _(sc_):
            act_ = nc.scalar.activation

            def step(i, s, t):
                def exps(b, p, heads):
                    if not known(b, 0, BATCHES):
                        return
                    for h in heads:
                        if h == 0:
                            wait(sc_, probst_mm, 4 * (b - 1))
                            wait(sc_, rsum_done, b - 1)
                        if h % (HEADS // 2) == 0:
                            wait(sc_, max_done, 2 * b + 2 * h // HEADS + 1)
                        ins = act_(probs[p][:, h * P:(h + 1) * P], clipped[p][:, h * P:(h + 1) * P], ACT.Exp,
                                   bias=negmax[p][:, h:h + 1], accum_out=sums[p][:, h:h + 1])
                        if h % PER == PER - 1:
                            ins.then_inc(exp_done, 1)

                def evacuate(g):
                    b = i - 1
                    if known(b, 0, BATCHES):
                        wait(sc_, probst_mm, 4 * b + g + 1)
                        wait(sc_, pv_mm, 4 * b + g - 1)
                        nc.scalar.copy(probst[g % 2][:, :], bank_t[g % 2][:, :]).then_inc(probst_done, 1)

                exps(i - 1, (s - 1) % 2, range(EARLY, HEADS))
                evacuate(0)
                evacuate(1)
                if known(i + 2, 0, BATCHES):
                    wait(sc_, xn1t_mm, i + 3)
                if known(i - 3, 0, BATCHES):
                    wait(sc_, xn2t_mm, i - 2)
                    wait(sc_, gate_mm, i - 4)
                    wait(sc_, xn2t_kept, i - 4)
                    nc.scalar.copy(xn2ts[(s - 3) % 2][:, :], xn2t_ps).then_inc(xn2t_done, 1)
                if known(i + 2, 0, BATCHES):
                    wait(sc_, kvq_mm, i + 1)
                    nc.scalar.copy(xn1t[s % 2][:, :], xn1t_ps).then_inc(xn1t_done, 1)
                exps(i, s % 2, range(0, PER))
                evacuate(2)
                exps(i, s % 2, range(PER, EARLY))
                evacuate(3)

            steps(sc_, step, STEPS_FROM, LOOP_FROM, LOOP_TO, STEPS_TO, 2)

            sc_.wait_ge(gate_done, BATCHES)
            act_(sig[:, :], logits[:, :], ACT.Sigmoid).then_inc(sig_done, 1)
            sc_.wait_ge(ffn_in, N_FFN)

            def shared(g, s, t):
                p = s % 2
                for c in range(CHUNKS):
                    wait(sc_, s_up_mm, 4 * g + c + 1)
                    if c == 0:
                        wait(sc_, s_down_mm, g - 1)
                    act_(s_act[p][:, c * SW:(c + 1) * SW], bank_s[:, c * 512:(c + 1) * 512], ACT.Gelu,
                         bias=s_upb[:, c:c + 1]).then_inc(s_gelu, 1)

            steps(sc_, shared, 0, 2, SGROUPS, SGROUPS, 2)

            def routed(j, s, t):
                p = s % 2
                wait(sc_, up_mm, j + 1)
                wait(sc_, down_mm, j - 1)
                for c in range(CHUNKS):
                    ins = act_(act[p][:, c * P:(c + 1) * P], bank_s[:, p * 512 + c * P:p * 512 + (c + 1) * P], ACT.Gelu,
                               bias=st_up[p][:, HIDDEN + c:HIDDEN + c + 1])
                ins.then_inc(gelu_done, 1)

            steps(sc_, routed, 0, 2, loop_end(2, TILES, TURN), TILES, TURN)

        @block.vector
        def _(dve):
            V = nc.vector
            own = [bass.AP(v[:, :].tensor, v[:, :].offset, [v[:, :].ap[0], [P + HD, HEADS], [1, HD]]) for v in val]
            dve.wait_ge(consts_in, N_CONSTS)
            dve.wait_ge(fills, 5)

            def step(i, s, t):
                b, p = i - 2, s % 2
                if known(b, 0, BATCHES):
                    wait(dve, recipt_mm, b + 1)
                    wait(dve, ot_done, b - 1)
                    V.tensor_copy(recipt[p][:, :], recipt_ps).then_inc(recipt_done, 1)
                    wait(dve, recipt_done, b + 1)
                    wait(dve, proj_mm, b - 1)
                wait(dve, stat2_done, min(i - 2, BATCHES) if isinstance(i, int) else i - 2)
                wait(dve, xn2_done, i - 4)
                if known(b, 0, BATCHES):
                    V.tensor_tensor(ot[p][:, :], ot_ps, recipt[p][:, :], ALU.mult).then_inc(ot_done, 1)
                if known(i - 3, 0, BATCHES):
                    p = (s - 3) % 2
                    V.bn_aggr(mv2[p][:, :], stat2[p][:, :]).then_inc(mv2_done, 1)
                b, p = i, s % 2
                if known(b, 0, BATCHES):
                    wait(dve, kvq_mm, b + 2)
                    wait(dve, pv_mm, 4 * (b - 1))
                    V.tensor_tensor(own[p],
                                    kv_v.rearrange("p (h d) -> p h d", d=HD),
                                    bv[:, :].rearrange("p (h d) -> p h d", d=HD), ALU.add).then_inc(v_done, 1)
                b, p = i + 1, (s + 1) % 2
                if known(b, 0, BATCHES):
                    wait(dve, kvq_mm, b + 1)
                    wait(dve, scores_mm, 2 * (b - 1))
                    for dst, src, bias, mask, n, done in ((km, kv_k, bk, kmask, PER, km_done),
                                                          (qm, kv_q, bq, qmask, GROUPS, qm_done)):
                        if done is qm_done:
                            wait(dve, mv1_done, i + 2)
                        V.scalar_tensor_tensor(dst[p][:, :].rearrange("p (n k) -> p n k", k=P),
                                               src.unsqueeze(1).to_broadcast([P, n, P]), bias[:, 0:1],
                                               mask[:, :].unsqueeze(2).to_broadcast([P, n, P]),
                                               op0=ALU.add, op1=ALU.mult).then_inc(done, 1)
                b, p = i + 3, (s + 3) % 2
                if known(b, 0, BATCHES):
                    if isinstance(b, int):
                        dve.wait_ge(x_in[b * XCHUNKS // BATCHES], 16)
                        wait(dve, mv1_done, b - 1)
                    elif s == LOOP_FROM:
                        for c in range(1, XCHUNKS):
                            dve.wait_ge(x_in[c], 16)
                    V.bn_stats(stat1[p][:, :], tok(x, b)).then_inc(stat1_done, 1)
                    wait(dve, stat1_done, b + 1)
                    wait(dve, xn1_done, b - 1)
                b, p = i + 2, s % 2
                if known(b, 0, BATCHES):
                    wait(dve, rstd1_done, b + 1)
                    wait(dve, xn1t_mm, b - 1)
                    V.tensor_scalar(xn1[p][:, :], tok(x, b), mv1[p][:, 0:1], rstd1[p][:, 0:1],
                                    ALU.subtract, ALU.mult).then_inc(xn1_done, 1)
                if known(i + 3, 0, BATCHES):
                    p = (s + 3) % 2
                    V.bn_aggr(mv1[p][:, :], stat1[p][:, :]).then_inc(mv1_done, 1)
                b, p = i - 3, (s - 3) % 2
                if known(b, 0, BATCHES):
                    wait(dve, rstd2_done, b + 1)
                    wait(dve, xn2t_mm, b - 1)
                    wait(dve, xn2_kept, b - 1)
                    V.tensor_scalar(xn2s[p][:, :], tok(x, b), mv2[p][:, 0:1], rstd2[p][:, 0:1],
                                    ALU.subtract, ALU.mult).then_inc(xn2_done, 1)
                b, p = i, s % 2
                if known(b, 0, BATCHES):
                    wait(dve, max_done, 2 * (b - 1))
                    wait(dve, exp_done, 4 * (b - 1))
                    for half in range(2):
                        at, n = half * HEADS // 2, HEADS // 2
                        wait(dve, scores_mm, 2 * b + half + 1)
                        V.tensor_scalar(clipped[p][:, at * P:(at + n) * P], bank_s[:, at * P:(at + n) * P],
                                        -CLAMP, CLAMP, ALU.max, ALU.min).then_inc(clip_done, 1)
                        wait(dve, clip_done, 2 * b + half + 1)
                        V.tensor_reduce(negmax[p][:, at:at + n],
                                        clipped[p][:, at * P:(at + n) * P].rearrange("p (h k) -> p h k", k=P), AX.X,
                                        ALU.max, negate=True).then_inc(max_done, 1)
                b, p = i - 1, (s - 1) % 2
                if known(b, 0, BATCHES):
                    wait(dve, exp_done, 4 * (b + 1))
                    wait(dve, recip_done, b - 1)
                    V.reciprocal(rsum[p][:, :], sums[p][:, :]).then_inc(rsum_done, 1)
                    wait(dve, rsum_done, b + 1)
                    wait(dve, recipt_mm, b - 1)
                    V.tensor_copy(recip[p][:, :].rearrange("p (h d) -> p h d", d=HD),
                                  rsum[p][:, :].unsqueeze(2).to_broadcast([P, HEADS, HD])).then_inc(recip_done, 1)
                b, p = i - 2, s % 2
                if known(b, 0, BATCHES):
                    wait(dve, proj_mm, b + 1)
                    if known(b - 1, 0, BATCHES):
                        wait(dve, gate_mm, b)
                    wait(dve, xb_done, b + 1)
                    V.tensor_tensor(tok(x, b), proj_ps, xb[p][:, :], ALU.add).then_inc(x1_done, 1)
                    wait(dve, x1_done, b + 1)
                    wait(dve, mv2_done, b - 1)
                b = i - 3
                if known(b, 0, BATCHES):
                    wait(dve, gate_mm, b + 1)
                    dst = logits[:, b * EXPERTS:(b + 1) * EXPERTS] if isinstance(b, int) else logits[:, bass.ds(b * EXPERTS, EXPERTS)]
                    V.tensor_tensor(dst, gate_ps, gate_b[:, :], ALU.add).then_inc(gate_done, 1)
                if known(i - 2, 0, BATCHES):
                    V.bn_stats(stat2[s % 2][:, :], tok(x, i - 2)).then_inc(stat2_done, 1)

            steps(dve, step, STEPS_FROM, LOOP_FROM, LOOP_TO, STEPS_TO, 2)

            count_of = [0]

            def do(ins):
                count_of[0] += 1
                ins.then_inc(route, 1)
                dve.wait_ge(route, count_of[0])

            def per_e(t):
                return t[:, :].unsqueeze(2).to_broadcast([P, BATCHES, EXPERTS])

            def per_t(t):
                return t[:, :].unsqueeze(1).to_broadcast([P, BATCHES, EXPERTS])

            dve.wait_ge(ffn_in, N_FFN)
            do(V.tensor_scalar(s_downb01[:, :], s_downb[:, :], 0.1, None, ALU.mult))
            dve.wait_ge(sig_done, 1)
            for k, scores in enumerate((sig, sig2)):
                do(V.tensor_reduce(best[k][:, :], by_e(scores), AX.X, ALU.max))
                do(V.tensor_tensor(by_e(eq), by_e(scores), per_e(best[k]), ALU.is_equal))
                do(V.tensor_tensor(by_e(sc), by_e(eq), per_t(rank_w), ALU.mult))
                do(V.tensor_reduce(win[:, :], by_e(sc), AX.X, ALU.max))
                do(V.tensor_tensor(by_e(oh[k]), by_e(sc), per_e(win), ALU.is_equal))
                if k == 0:
                    do(V.scalar_tensor_tensor(sig2[:, :], oh[0][:, :], -4.0, sig[:, :], op0=ALU.mult, op1=ALU.add))
            do(V.tensor_tensor(both[:, :], oh[0][:, :], oh[1][:, :], ALU.add))
            V.tensor_copy(eq[:, 0:1], both[:, 0:1]).then_inc(chosen, 1)
            dve.wait_ge(chosen, 1)
            do(V.scalar_tensor_tensor(den[:, :], best[0][:, :], 1e-6, best[1][:, :], op0=ALU.add, op1=ALU.add))
            do(V.reciprocal(rden[:, :], den[:, :]))
            for k in range(TOPK):
                do(V.tensor_tensor(weight[k][:, :], best[k][:, :], rden[:, :], ALU.mult))

            dve.wait_ge(rank_mm, 1)
            do(V.memset(pre_a[:, 0:EXPERTS], 0.0))
            do(V.tensor_copy(pre_a[:, EXPERTS:RE], bank_b[:, 0:RE - EXPERTS]))
            src, dst, d = pre_a, pre_b, EXPERTS
            while d < RE:
                do(V.tensor_copy(dst[:, 0:d], src[:, 0:d]))
                do(V.tensor_tensor(dst[:, d:RE], src[:, d:RE], src[:, 0:RE - d], ALU.add))
                src, dst, d = dst, src, 2 * d
            before = src
            first, total = count[:, 0:EXPERTS], base_a[:, 0:EXPERTS]
            do(V.tensor_copy(first, before[:, PART[1] * EXPERTS:(PART[1] + 1) * EXPERTS]))
            do(V.tensor_tensor(total, before[:, RE - EXPERTS:RE], bank_b[:, RE - EXPERTS:RE], ALU.add))
            do(V.tensor_tensor(count[:, EXPERTS:SETS], total, first, ALU.subtract))
            do(V.tensor_scalar(count_i[:, :], count[:, :], float(P - 1), None, ALU.add))
            do(V.tensor_scalar(count_j[:, :], count_i[:, :], 7, 7, ALU.logical_shift_right, ALU.logical_shift_left))
            do(V.tensor_copy(padded[:, :], count_j[:, :]))
            do(V.tensor_copy(base_a[:, :], padded[:, :]))
            src, dst, d = base_a, base_b, 1
            while d < EXPERTS:
                do(V.tensor_copy(by_e(dst)[:, :, 0:d], by_e(src)[:, :, 0:d]))
                do(V.tensor_tensor(by_e(dst)[:, :, d:EXPERTS], by_e(src)[:, :, d:EXPERTS],
                                   by_e(src)[:, :, 0:EXPERTS - d], ALU.add))
                src, dst, d = dst, src, 2 * d
            do(V.tensor_copy(ends[:, :], src[:, :]))
            do(V.tensor_tensor(starts[:, :], ends[:, :], padded[:, :], ALU.subtract))
            do(V.tensor_tensor(starts[:, EXPERTS:SETS], starts[:, EXPERTS:SETS], first, ALU.subtract))
            do(V.tensor_tensor(slot_of[:, :], before[:, :], bank_a[:, 0:RE], ALU.add))
            for p in range(PARTS):
                n = PART[p + 1] - PART[p]
                do(V.tensor_tensor(by_e(sig2)[:, PART[p]:PART[p + 1], :], by_e(slot_of)[:, PART[p]:PART[p + 1], :],
                                   by_e(starts)[:, p:p + 1, :].to_broadcast([P, n, EXPERTS]), ALU.add))
            for k in range(TOPK):
                do(V.tensor_tensor(sc[:, :], sig2[:, :], oh[k][:, :], ALU.mult))
                do(V.tensor_reduce(slot_f[k][:, :], by_e(sc), AX.X, ALU.add))
                do(V.tensor_copy(slot[k][:, :], slot_f[k][:, :]))
            V.tensor_copy(eq[:, 1:2], ends[:, 0:1]).then_inc(slots_done, 1)
            for p in range(PARTS):
                lo, hi = PTILE[p], PTILE[p + 1]
                do(V.tensor_tensor(by_e(passed)[:, lo:hi, :],
                                   by_e(ends)[:, p:p + 1, :].to_broadcast([P, hi - lo, EXPERTS]),
                                   tile_at[:, lo:hi].unsqueeze(2).to_broadcast([P, hi - lo, EXPERTS]), ALU.is_le))
            do(V.tensor_reduce(expert_f[:, :], passed[:, :].rearrange("p (j e) -> p j e", e=EXPERTS), AX.X, ALU.add))
            do(V.tensor_scalar(expert_g[:, :], expert_f[:, :], float(EXPERTS - 1), None, ALU.min))
            do(V.tensor_copy(expert[:, :], expert_g[:, :]))

            def shared(g, s, t):
                p = s % 2
                xg = tok(x, g * SG, SG)
                V.tensor_tensor(xg.rearrange("p (b c) -> p b c", c=P), xg.rearrange("p (b c) -> p b c", c=P),
                                s_downb01[:, :].unsqueeze(1).to_broadcast([P, SG, P]), ALU.add).then_inc(s_bias, 1)
                wait(dve, s_bias, g + 1)
                wait(dve, s_down_mm, g + 1)
                V.scalar_tensor_tensor(xg, bank_t[p][:, :], 0.1, xg, op0=ALU.mult, op1=ALU.add).then_inc(s_added, 1)

            steps(dve, shared, 0, 2, SGROUPS, SGROUPS, 2)

            def routed(j, s, t):
                b = j + 1
                if known(b, 0, TILES):
                    at = expert[0:1, b:b + 1] if isinstance(b, int) else expert[0:1, bass.ds(b, 1)]
                    its_expert = V.value_load(at, min_val=0, max_val=EXPERTS - 1)
                b, p = j - 2, s % 2
                if known(b, 0, TILES):
                    n = (s - 2) % RING
                    wait(dve, down_mm, b + 1)
                    if not isinstance(b, int) or b >= RING:
                        dve.wait_ge(y_out[n], use_of(s - 2, t) * 16)
                    V.tensor_tensor(y[n][:, :], bank_t[p][:, 0:P], st_down[n][:, HIDDEN:DNW],
                                    ALU.add).then_inc(y_done, 1)
                b, p = j + 1, (s + 1) % 2
                if known(b, 0, TILES):
                    wait(dve, xst_mm, b + 1)
                    wait(dve, up_mm, b - 1)
                    V.tensor_copy(xst[p][:, :], (bank_a, bank_b)[p][:, 0:P]).then_inc(xst_done, 1)
                    wait(dve, gelu_done, b - 1)
                    V.tensor_copy(st_up[p][:, :], up_w[:, bass.ds(its_expert * UPW, UPW)]).then_inc(up_w_done, 1)
                    wait(dve, y_done, b - RING + 1)
                    V.tensor_copy(st_down[(s + 1) % RING][:, :],
                                  down_w[:, bass.ds(its_expert * DNW, DNW)]).then_inc(down_w_done, 1)

            steps(dve, routed, -1, 7, loop_end(7, TILES - 1, TURN), TILES + 2, TURN)

            for t in range(BATCHES):
                p = t % 2
                if t % YGROUP == 0:
                    dve.wait_ge(y_in[t // YGROUP], 16 * TOPK * YGROUP)
                if t >= 2:
                    dve.wait_ge(summed, t - 1)
                V.scalar_tensor_tensor(part[p][:, :], tok(yg[0], t), weight[0][:, t:t + 1], tok(x, t),
                                       op0=ALU.mult, op1=ALU.add).then_inc(half_sum, 1)
                dve.wait_ge(half_sum, t + 1)
                V.scalar_tensor_tensor(tok(x, t), tok(yg[1], t), weight[1][:, t:t + 1], part[p][:, :],
                                       op0=ALU.mult, op1=ALU.add).then_inc(summed, 1)


def kernel(x, ctx_768, L0_xattn_Wq, L0_xattn_bq, L0_xattn_Wk, L0_xattn_bk, L0_xattn_Wv, L0_xattn_bv,
           L0_xattn_Wo, L0_xattn_bo, L0_ffn_gate_w, L0_ffn_gate_bias, L0_ffn_Wu, L0_ffn_bu, L0_ffn_Wd,
           L0_ffn_bd, L0_ffn_sWu, L0_ffn_sbu, L0_ffn_sWd, L0_ffn_sbd):
    import concourse.bacc as bacc
    import numpy as np
    from concourse.bass_utils import run_bass_kernel_spmd

    def rows_of(w):
        w = np.asarray(w)
        w = w.reshape(w.shape[:-1] + (CHUNKS, P))
        order = (w.ndim - 1,) + tuple(range(w.ndim - 3)) + (w.ndim - 2, w.ndim - 3)
        return w.transpose(order)

    def packed(parts, arrays_of):
        values = [np.atleast_2d(np.asarray(arrays_of[name])) for name, _ in parts]
        whole = np.zeros((max(v.shape[0] for v in values), sum(w for _, w in parts)), np.float32)
        at = 0
        for v, (_, w) in zip(values, parts):
            whole[:v.shape[0], at:at + w] = v
            at += w
        return whole

    part = np.arange(P)
    data = {
        "x": x,
        "ctxt": np.asarray(ctx_768).transpose(2, 0, 1).reshape(CTX, TOKENS),
        "cols": packed(COLS, {
            "wq": L0_xattn_Wq, "wk": L0_xattn_Wk, "wv": L0_xattn_Wv, "wo": L0_xattn_Wo,
            "gate_w": np.asarray(L0_ffn_gate_w).transpose(1, 0), "ident": np.eye(P),
            "tri": np.triu(np.ones((P, P)), 1),
            "qmask": (part[:, None] // (P // GROUPS) == np.arange(GROUPS)) * HD ** -0.5,
            "kmask": part[:, None] // HD % PER == np.arange(PER),
            "bq": np.asarray(L0_xattn_bq).reshape(P, 1), "bk": np.asarray(L0_xattn_bk).reshape(P, 1)}),
        "rows": packed(ROWS, {
            "bv": L0_xattn_bv, "bo": L0_xattn_bo, "gate_b": L0_ffn_gate_bias,
            "rank_w": np.arange(EXPERTS, 0, -1), "tile_at": np.concatenate([np.arange(PTILE[p + 1] - PTILE[p]) for p in range(PARTS)]) * P})[0],
        "up": np.concatenate([np.asarray(L0_ffn_Wu).transpose(2, 0, 1),
                              np.asarray(L0_ffn_bu).reshape(EXPERTS, CHUNKS, P).transpose(2, 0, 1)],
                             axis=2).reshape(P, EXPERTS * UPW),
        "down": rows_of(L0_ffn_Wd).reshape(P, EXPERTS * HIDDEN),
        "downb": L0_ffn_bd,
        "s_up": np.asarray(L0_ffn_sWu).transpose(1, 0),
        "s_upb": np.asarray(L0_ffn_sbu).reshape(CHUNKS, P).transpose(1, 0),
        "s_down": rows_of(L0_ffn_sWd).reshape(P, HIDDEN),
        "s_downb": L0_ffn_sbd,
    }
    nc = bacc.Bacc("TRN2", target_bir_lowering=False, num_devices=1)
    arrays, dr = {}, {}
    for name, a in data.items():
        arrays[f"in_{name}"] = np.ascontiguousarray(a)
        dr[name] = nc.dram_tensor(f"in_{name}", arrays[f"in_{name}"].shape, F32, kind="ExternalInput").ap()
    out = nc.dram_tensor("out_dram", (BATCHES, P, P), F32, kind="ExternalOutput").ap()
    xattn_moe(nc, dr, out)
    return run_bass_kernel_spmd(nc, [arrays], core_ids=[0]).results[0]["out_dram"]
```

```python
from contextlib import ExitStack

import concourse.bass as bass
from concourse import mybir

F32 = mybir.dt.float32
BF16 = mybir.dt.bfloat16
I32 = mybir.dt.int32
U32 = mybir.dt.uint32
ALU = mybir.AluOpType
ACT = mybir.ActivationFunctionType
AX = mybir.AxisListType

P = 128
BATCHES = 32
CTX = 96
HEADS = 16
HD = P // HEADS
GROUPS = 4
PER = HEADS // GROUPS
CLAMP = 10000.0
EPS = 1e-5
TOKENS = BATCHES * P
EXPERTS = 8
TOPK = 2
CHUNKS = 4
HIDDEN = CHUNKS * P
PARTS = 2
PART = (0, 22, BATCHES)
PTILE = tuple(TOPK * b + p * (EXPERTS - 1) for p, b in enumerate(PART))
TILES = PTILE[PARTS]
UPW = HIDDEN + CHUNKS
DNW = HIDDEN + P
SG = 4
SGROUPS = BATCHES // SG
SW = SG * P
MIDDLE = 2
FRONT = 5
SCATTERS = (3, 3, 3, 3, 3, 1)
RING = 4
STORE_LAG = 7
TURN = 8
YGROUP = 2
XCHUNKS = 4
EARLY = 2
LOOP_FROM, LOOP_TO = 6, 28
COLS = (("wq", P), ("wk", P), ("wv", P), ("wo", P), ("gate_w", EXPERTS), ("ident", P), ("tri", P),
        ("qmask", GROUPS), ("kmask", PER), ("bq", 1), ("bk", 1))
ROWS = (("bv", P), ("bo", P), ("gate_b", EXPERTS), ("rank_w", EXPERTS), ("tile_at", TILES))
STEPS_FROM, STEPS_TO = -3, BATCHES + 3


def wait(eng, sem, count):
    if not isinstance(count, int) or count > 0:
        eng.wait_ge(sem, count)


def known(i, lo, hi):
    return not isinstance(i, int) or lo <= i < hi


def steps(eng, body, first, loop_from, loop_to, last, unroll):
    for i in range(first, loop_from):
        body(i, i, 0)
    with eng.Fori(0, (loop_to - loop_from) // unroll) as t:
        for u in range(unroll):
            body(t * unroll + (loop_from + u), loop_from + u, t)
    for i in range(loop_to, last):
        body(i, i, 0)


def use_of(s, t):
    return t * (TURN // RING) + s // RING


def part_of(i, bounds):
    return max(p for p in range(PARTS) if i >= bounds[p])


def loop_end(start, end, unroll):
    return start + (end - start) // unroll * unroll


def xattn_moe(nc, dr, out):
    ctx_stack = ExitStack()
    with ctx_stack:
        def sb(name, shape, dt=F32):
            return ctx_stack.enter_context(nc.sbuf_tensor(name, shape, dt))

        def psum(name, width):
            return ctx_stack.enter_context(nc.psum_tensor(name, [P, width], F32))

        def sem(name):
            return ctx_stack.enter_context(nc.semaphore(name))

        cols, rows = sb("cols", [P, sum(w for _, w in COLS)]), sb("rows", [P, sum(w for _, w in ROWS)])

        def piece(t, parts, name):
            names = [n for n, _ in parts]
            at = sum(w for _, w in parts[:names.index(name)])
            return t[:, at:at + parts[names.index(name)][1]]

        wq, wk, wv, wo, gate_w, ident, tri, qmask, kmask, bq, bk = (piece(cols, COLS, n) for n, _ in COLS)
        wk, wv = wk[0:CTX, :], wv[0:CTX, :]
        bv, bo, gate_b, rank_w, tile_at = (piece(rows, ROWS, n) for n, _ in ROWS)
        ones, tri_b = sb("ones", [P, P], BF16), sb("tri_b", [P, P], BF16)
        up_w = sb("up_w", [P, EXPERTS * UPW])
        down_w = sb("down_w", [P, EXPERTS * DNW])
        s_up, s_upb, s_down = sb("s_up", [P, HIDDEN]), sb("s_upb", [P, CHUNKS]), sb("s_down", [P, HIDDEN])
        s_downb, s_downb01 = sb("s_downb", [P, P]), sb("s_downb01", [P, P])
        minus_half, eps = sb("minus_half", [P, 1]), sb("eps", [P, 1])
        zero = sb("zero", [P, P])

        x = sb("x", [P, TOKENS])
        xn2 = sb("xn2", [P, TOKENS])
        xn2t = sb("xn2t", [P, TOKENS])
        logits = sb("logits", [P, BATCHES * EXPERTS])

        def two(name, shape, dt=F32):
            return [sb(f"{name}{n}", shape, dt) for n in range(2)]

        ctxt = two("ctxt", [CTX, P])
        xn1, xn1t = two("xn1", [P, P]), two("xn1t", [P, P])
        stat1, mv1, ve1, rstd1 = two("stat1_", [P, 6]), two("mv1_", [P, 2]), two("ve1_", [P, 1]), two("rstd1_", [P, 1])
        stat2, mv2, ve2, rstd2 = two("stat2_", [P, 6]), two("mv2_", [P, 2]), two("ve2_", [P, 1]), two("rstd2_", [P, 1])
        km, qm = two("km", [P, PER * P]), two("qm", [P, GROUPS * P])
        val = two("val", [P, HEADS * P])
        clipped, probs = two("clipped", [P, HEADS * P]), two("probs", [P, HEADS * P])
        negmax, sums, rsum = two("negmax", [P, HEADS]), two("sums", [P, HEADS]), two("rsum", [P, HEADS])
        recip, recipt = two("recip", [P, P]), two("recipt", [P, P])
        probst = two("probst", [P, PER * P])
        ot, xb = two("ot", [P, P]), two("xb", [P, P])
        xn2s, xn2ts = two("xn2s", [P, P]), two("xn2ts", [P, P])

        bank_s = psum("bank_s", GROUPS * 512)
        bank_t = [psum(f"bank_t{n}", 512) for n in range(2)]
        bank_a, bank_b = psum("bank_a", 512), psum("bank_b", 512)
        kv_k, kv_v, kv_q = bank_a[:, 0:P], bank_a[:, P:2 * P], bank_a[:, 2 * P:3 * P]
        proj_ps, gate_ps = bank_a[:, 0:P], bank_a[:, P:P + EXPERTS]
        xn1t_ps, xn2t_ps = bank_a[:, 0:P], bank_a[:, P:2 * P]
        rank_ps = bank_a
        ot_ps, recipt_ps = bank_b[:, 0:P], bank_b[:, P:2 * P]

        consts_in = sem("consts_in")
        shared_in, ffn_in = sem("shared_in"), sem("ffn_in")
        x_in = [sem(f"x_in{n}") for n in range(XCHUNKS)]
        ctx_in = [sem(f"ctx_in{n}") for n in range(2)]
        fills = sem("fills")
        zeroed = sem("zeroed")
        slots_zeroed = sem("slots_zeroed")
        stat1_done, mv1_done, ve1_done, rstd1_done = sem("stat1_done"), sem("mv1_done"), sem("ve1_done"), sem("rstd1_done")
        stat2_done, mv2_done, ve2_done, rstd2_done = sem("stat2_done"), sem("mv2_done"), sem("ve2_done"), sem("rstd2_done")
        xn1_done, xn1t_mm, xn1t_done = sem("xn1_done"), sem("xn1t_mm"), sem("xn1t_done")
        kvq_mm, v_done, km_done, qm_done = sem("kvq_mm"), sem("v_done"), sem("km_done"), sem("qm_done")
        scores_mm, clip_done, max_done = sem("scores_mm"), sem("clip_done"), sem("max_done")
        exp_done = sem("exp_done")
        probst_mm, probst_done, pv_mm = sem("probst_mm"), sem("probst_done"), sem("pv_mm")
        rsum_done = sem("rsum_done")
        recip_done, recipt_mm, recipt_done, ot_done = sem("recip_done"), sem("recipt_mm"), sem("recipt_done"), sem("ot_done")
        proj_mm, xb_done, x1_done = sem("proj_mm"), sem("xb_done"), sem("x1_done")
        xn2_done, xn2t_mm, xn2t_done = sem("xn2_done"), sem("xn2t_mm"), sem("xn2t_done")
        gate_mm, gate_done = sem("gate_mm"), sem("gate_done")
        xn2_kept, xn2t_kept = sem("xn2_kept"), sem("xn2t_kept")

        sig_done, route = sem("sig_done"), sem("route")
        chosen, rank_mm, ranks_read, slots_done = sem("chosen"), sem("rank_mm"), sem("ranks_read"), sem("slots_done")
        scattered = [sem(f"scattered{p}") for p in range(PARTS)]
        s_up_mm, s_gelu = sem("s_up_mm"), sem("s_gelu")
        s_down_mm, s_bias, s_added = sem("s_down_mm"), sem("s_bias"), sem("s_added")
        xs_in = [sem(f"xs_in{n}") for n in range(RING)]
        xst_mm, xst_done, up_w_done, down_w_done = sem("xst_mm"), sem("xst_done"), sem("up_w_done"), sem("down_w_done")
        up_mm, gelu_done, down_mm, y_done = sem("up_mm"), sem("gelu_done"), sem("down_mm"), sem("y_done")
        y_out = [sem(f"y_out{n}") for n in range(RING)]
        y_in = [sem(f"y_in{n}") for n in range(BATCHES // YGROUP)]
        half_sum, summed = sem("half_sum"), sem("summed")
        stored = sem("stored")

        RE = BATCHES * EXPERTS
        sig, sig2, eq, sc = (sb(n, [P, RE]) for n in ("sig", "sig2", "eq", "sc"))
        oh = [sb(f"oh{k}", [P, RE]) for k in range(TOPK)]
        both = [sb(f"both{p}", [P, (PART[p + 1] - PART[p] + 1) * EXPERTS], BF16) for p in range(PARTS)]
        best = [sb(f"best{k}", [P, BATCHES]) for k in range(TOPK)]
        win, den, rden = (sb(n, [P, BATCHES]) for n in ("win", "den", "rden"))
        weight = [sb(f"weight{k}", [P, BATCHES]) for k in range(TOPK)]
        slot_f = [sb(f"slot_f{k}", [P, BATCHES]) for k in range(TOPK)]
        slot = [sb(f"slot{k}", [P, BATCHES], I32) for k in range(TOPK)]
        padded, base_a, base_b, starts = (sb(n, [P, EXPERTS]) for n in ("padded", "base_a", "base_b", "starts"))
        count_i, count_j = sb("count_i", [P, EXPERTS], I32), sb("count_j", [P, EXPERTS], I32)
        ranks = sb("ranks", [P, RE + EXPERTS])
        passed = sb("passed", [P, TILES * EXPERTS])
        expert_f, expert_g = sb("expert_f", [P, TILES]), sb("expert_g", [P, TILES])
        expert = sb("expert", [P, TILES], I32)
        s_act = two("s_act", [P, CHUNKS * SW])
        def carved(buffer, at, width, n=1):
            return [buffer[:, at + k * width:at + (k + 1) * width] for k in range(n)]

        xs, act, xst, part = (carved(probs[0], 0, P, RING), carved(probs[0], RING * P, HIDDEN, 2),
                              carved(probs[0], RING * P + 2 * HIDDEN, P, 2),
                              carved(probs[0], (RING + 2) * P + 2 * HIDDEN, P, 2))
        st_up, y = carved(probs[1], 0, UPW, 2), carved(probs[1], 2 * UPW, P, RING)
        st_down = [clipped[n // 2][:, n % 2 * DNW:(n % 2 + 1) * DNW] for n in range(RING)]

        slots_x, slots_y = ([nc.dram_tensor(f"{name}{p}", ((PTILE[p + 1] - PTILE[p]) * P, P), F32).ap()
                             for p in range(PARTS)] for name in ("slots_x", "slots_y"))

        def tok(t, b, n=1):
            return t[:, bass.ds(b * P, n * P)] if not isinstance(b, int) else t[:, b * P:(b + n) * P]

        def gathered(k, t):
            return tok(xn2, t) if k == 0 else tok(val[t * 2 // BATCHES], t % (BATCHES // 2))

        def by_e(t):
            return t[:, :].rearrange("p (t e) -> p t e", e=EXPERTS)

        N_CONSTS = 16 * 2
        N_SHARED = 16 * 4
        N_FFN = 16 * (1 + 2 * EXPERTS)
        ZEROINGS = 4

        block = ctx_stack.enter_context(nc.Block())

        @block.sync
        def _(sp):
            xv = dr["x"].rearrange("b s c -> s b c")
            n = BATCHES // XCHUNKS

            def load_x(c):
                sp.dma_start(tok(x, c * n, n).rearrange("p (b c) -> p b c", c=P),
                             xv[:, c * n:(c + 1) * n, :]).then_inc(x_in[c], 16)

            def load_ctx(b, s, t):
                wait(sp, kvq_mm, b)
                src = dr["ctxt"][:, b * P:(b + 1) * P] if isinstance(b, int) else dr["ctxt"][:, bass.ds(b * P, P)]
                sp.dma_start(ctxt[s % 2][:, :], src).then_inc(ctx_in[s % 2], 16)

            sp.dma_start(cols[:, :], dr["cols"]).then_inc(consts_in, 16)
            load_x(0)
            sp.dma_start(rows[:, :], dr["rows"].partition_broadcast(P)).then_inc(consts_in, 16)
            load_ctx(0, 0, 0)
            load_ctx(1, 1, 0)
            for c in range(1, XCHUNKS):
                load_x(c)
            for e in range(EXPERTS):
                with sp.Fori(2 * e + 1, min(2 * e + 3, BATCHES // 2)) as t:
                    load_ctx(t * 2, 0, t)
                    load_ctx(t * 2 + 1, 1, t)
                sp.dma_start(up_w[:, e * UPW:(e + 1) * UPW], dr["up"][:, e * UPW:(e + 1) * UPW]).then_inc(ffn_in, 16)
                sp.dma_start(down_w[:, e * DNW:e * DNW + HIDDEN],
                             dr["down"][:, e * HIDDEN:(e + 1) * HIDDEN]).then_inc(ffn_in, 16)
                if e == 0:
                    sp.wait_ge(zeroed, 1)
                if e < ZEROINGS:
                    for p in range(PARTS):
                        lo = max(e * TILES // ZEROINGS, PTILE[p]) - PTILE[p]
                        hi = min((e + 1) * TILES // ZEROINGS, PTILE[p + 1]) - PTILE[p]
                        if lo < hi:
                            sp.dma_start(slots_x[p][lo * P:hi * P, :].rearrange("(t p) c -> p t c", p=P),
                                         zero[:, :].unsqueeze(1).to_broadcast([P, hi - lo, P])).then_inc(slots_zeroed, 16)
                if e == 1:
                    for dst, src in ((s_up, dr["s_up"]), (s_down, dr["s_down"]), (s_upb, dr["s_upb"]),
                                     (s_downb, dr["s_downb"].partition_broadcast(P))):
                        sp.dma_start(dst[:, :], src).then_inc(shared_in, 16)
            dnv = down_w[:, :].rearrange("p (e w) -> p e w", w=DNW)
            sp.dma_start(dnv[:, :, HIDDEN:DNW], dr["downb"].partition_broadcast(P)).then_inc(ffn_in, 16)

            def slot_rows(parts, j, s):
                p = part_of(s, PTILE)
                j = j - PTILE[p]
                return parts[p][j * P:(j + 1) * P, :] if isinstance(j, int) else parts[p][bass.ds(j * P, P), :]

            def tile_io(j, s, t):
                if known(j, 0, TILES):
                    wait(sp, xst_mm, j - RING + 1)
                    sp.dma_start(xs[s % RING][:, :], slot_rows(slots_x, j, s)).then_inc(xs_in[s % RING], 16)
                b, n = j - STORE_LAG, (s - STORE_LAG) % RING
                if known(b, 0, TILES):
                    wait(sp, y_done, b + 1)
                    sp.dma_start(slot_rows(slots_y, b, s - STORE_LAG), y[n][:, :]).then_inc(y_out[n], 16)

            sp.wait_ge(probst_mm, 4 * BATCHES)
            for p in range(PARTS):
                sp.wait_ge(scattered[p], 16 * TOPK * (PART[p + 1] - PART[p]))
                start = PTILE[p] + STORE_LAG
                steps(sp, tile_io, PTILE[p], start, loop_end(start, PTILE[p + 1], RING),
                      PTILE[p + 1] + (STORE_LAG if p == PARTS - 1 else 0), RING)

            ov = out.rearrange("b s c -> s b c")
            bounds = list(range(0, FRONT * SG, SG)) + list(range(FRONT * SG, BATCHES + 1, YGROUP))
            for lo, hi in zip(bounds, bounds[1:]):
                sp.wait_ge(summed, hi)
                sp.dma_start(ov[:, lo:hi, :],
                             tok(x, lo, hi - lo).rearrange("p (b c) -> p b c", c=P)).then_inc(stored, 16)
            sp.wait_ge(stored, 16 * (len(bounds) - 1))

        @block.gpsimd
        def _(pool):
            nc.gpsimd.memset(minus_half[:, :], -0.5).then_inc(fills, 1)
            nc.gpsimd.memset(eps[:, :], EPS).then_inc(fills, 1)
            nc.gpsimd.memset(zero[:, :], 0.0).then_inc(zeroed, 1)
            nc.gpsimd.memset(ones[:, :], 1.0).then_inc(fills, 1)
            for v in val:
                nc.gpsimd.memset(v[:, :], 0.0).then_inc(fills, 1)
            pool.wait_ge(fills, 5)
            pool.wait_ge(consts_in, N_CONSTS)

            def rstd(b, mv, ve, out_, mv_done, ve_done, done, used, s):
                wait(pool, mv_done, b + 1)
                wait(pool, used, b - 1)
                nc.gpsimd.tensor_tensor(ve[s][:, :], mv[s][:, 1:2], eps[:, :], ALU.add).then_inc(ve_done, 1)
                wait(pool, ve_done, b + 1)
                nc.gpsimd.tensor_tensor(out_[s][:, :], ve[s][:, :], minus_half[:, :], ALU.pow).then_inc(done, 1)

            def step(i, s, t):
                if known(i - 3, 0, BATCHES):
                    rstd(i - 3, mv2, ve2, rstd2, mv2_done, ve2_done, rstd2_done, xn2_done, (s - 3) % 2)
                if known(i + 3, 0, BATCHES):
                    rstd(i + 3, mv1, ve1, rstd1, mv1_done, ve1_done, rstd1_done, xn1_done, (s + 3) % 2)
                b = i - 1
                if known(b, 0, BATCHES):
                    wait(pool, x1_done, b - 1)
                    nc.gpsimd.tensor_tensor(xb[(s - 1) % 2][:, :], tok(x, b), bo[:, :], ALU.add).then_inc(xb_done, 1)
                b, p = i - 3, (s - 3) % 2
                if known(b, 0, BATCHES):
                    wait(pool, xn2_done, b + 1)
                    nc.gpsimd.tensor_copy(tok(xn2, b), xn2s[p][:, :]).then_inc(xn2_kept, 1)
                    wait(pool, xn2t_done, b + 1)
                    nc.gpsimd.tensor_copy(tok(xn2t, b), xn2ts[p][:, :]).then_inc(xn2t_kept, 1)

            steps(pool, step, STEPS_FROM, LOOP_FROM, LOOP_TO, LOOP_TO, 2)

            def scatter(lo, hi):
                for t in range(lo, hi):
                    for k in range(TOPK):
                        nc.gpsimd.indirect_dma_start(
                            out=slots_x[part_of(t, PART)],
                            out_offset=bass.IndirectOffsetOnAxis(ap=slot[k][:, t:t + 1].bitcast(U32), axis=0),
                            in_=tok(xn2, t), in_offset=None).then_inc(scattered[part_of(t, PART)], 16)

            pool.wait_ge(slots_zeroed, 16 * (ZEROINGS + PARTS - 1))
            pool.wait_ge(xn2_kept, PART[1])
            pool.wait_ge(slots_done, 1)
            scatter(0, SCATTERS[0])
            for n, i in enumerate(range(LOOP_TO, STEPS_TO)):
                step(i, i, 0)
                scatter(sum(SCATTERS[:n + 1]), sum(SCATTERS[:n + 2]))
            scatter(sum(SCATTERS), PART[1])
            pool.wait_ge(slots_done, 2)
            pool.wait_ge(xn2_kept, BATCHES)
            scatter(PART[1], BATCHES)
            for p in range(PARTS):
                pool.wait_ge(scattered[p], 16 * TOPK * (PART[p + 1] - PART[p]))
                for n in range(RING):
                    pool.wait_ge(y_out[n], 16 * len(range(n, PTILE[p + 1], RING)))
                for t in range(PART[p], PART[p + 1]):
                    for k in range(TOPK):
                        nc.gpsimd.indirect_dma_start(
                            out=gathered(k, t), out_offset=None, in_=slots_y[p],
                            in_offset=bass.IndirectOffsetOnAxis(ap=slot[k][:, t:t + 1].bitcast(U32), axis=0),
                        ).then_inc(y_in[t // YGROUP], 16)

        @block.tensor
        def _(pe):
            mm, tr = nc.tensor.matmul, nc.tensor.transpose
            pe.wait_ge(consts_in, N_CONSTS)
            pe.wait_ge(fills, 5)

            def step(i, s, t):
                b, p = i + 1, (s + 1) % 2
                if known(b, 0, BATCHES) or known(i, 0, BATCHES):
                    wait(pe, qm_done, min(b, BATCHES) if isinstance(b, int) else b)
                    wait(pe, v_done, i)
                    wait(pe, x1_done, b - 3)
                    wait(pe, gate_done, b - 4)
                    wait(pe, xn1t_done, min(b + 1, BATCHES) if isinstance(b, int) else b + 1)
                if known(i, 0, BATCHES):
                    last = mm(kv_v, ctxt[s % 2][:, :], wv[:, :], start=True, stop=True)
                if known(b, 0, BATCHES):
                    pe.wait_ge(ctx_in[p], (t + (s + 1) // 2 + 1) * 16)
                    mm(kv_k, wk[:, :], ctxt[p][:, :], start=True, stop=True)
                    last = mm(kv_q, wq[:, :], xn1t[p][:, :], start=True, stop=True)
                if known(b, 0, BATCHES) or known(i, 0, BATCHES):
                    last.then_inc(kvq_mm, 1)
                b, p = i - 1, (s - 1) % 2

                def turn(g):
                    if isinstance(i, int) and i == LOOP_TO and g == 0:
                        pe.wait_ge(s_added, MIDDLE)
                    wait(pe, exp_done, 4 * b + g + 1)
                    wait(pe, probst_done, 4 * b + g - 1)
                    for r in range(PER):
                        h = g * PER + r
                        last = tr(bank_t[g % 2][:, r * P:(r + 1) * P], probs[p][:, h * P:(h + 1) * P], ident[:, :])
                    last.then_inc(probst_mm, 1)

                def weigh(g):
                    wait(pe, probst_done, 4 * b + g + 1)
                    if g == 0:
                        wait(pe, v_done, b + 1)
                        wait(pe, ot_done, b)
                    for r in range(PER):
                        h = g * PER + r
                        last = mm(ot_ps, val[p][:, h * P:(h + 1) * P], probst[g % 2][:, r * P:(r + 1) * P],
                                  start=(h == 0), stop=(h == HEADS - 1))
                    last.then_inc(pv_mm, 1)

                for half in range(2):
                    if known(i, 0, BATCHES):
                        if half == 0:
                            wait(pe, qm_done, i + 1)
                        wait(pe, clip_done, 2 * (i - 1) + half + 1)
                        for j in range(half * GROUPS // 2, (half + 1) * GROUPS // 2):
                            last = mm(bank_s[:, j * 512:(j + 1) * 512], qm[s % 2][:, j * P:(j + 1) * P],
                                      km[s % 2][:, :], start=True, stop=True)
                        last.then_inc(scores_mm, 1)
                    if known(b, 0, BATCHES):
                        turn(half)
                if known(i + 2, 0, BATCHES) or known(i - 3, 0, BATCHES):
                    wait(pe, v_done, min(i + 1, BATCHES) if isinstance(i, int) else i + 1)
                    wait(pe, qm_done, min(i + 2, BATCHES) if isinstance(i, int) else i + 2)
                    if isinstance(i, int) and i >= BATCHES:
                        wait(pe, x1_done, i - 2)
                        wait(pe, gate_done, i - 3)
                if known(i - 3, 0, BATCHES):
                    wait(pe, xn2_done, i - 2)
                    tr(xn2t_ps, xn2s[(s - 3) % 2][:, :], ident[:, :]).then_inc(xn2t_mm, 1)
                if known(i + 2, 0, BATCHES):
                    wait(pe, xn1_done, i + 3)
                    tr(xn1t_ps, xn1[s % 2][:, :], ident[:, :]).then_inc(xn1t_mm, 1)
                if known(b, 0, BATCHES):
                    weigh(0)
                    turn(2)
                    weigh(1)
                    turn(3)
                if known(i - 2, 0, BATCHES) or known(i - 3, 0, BATCHES):
                    wait(pe, xn1t_done, min(i + 3, BATCHES) if isinstance(i, int) else i + 3)
                    wait(pe, xn2t_done, i - 2)
                if known(i - 2, 0, BATCHES):
                    wait(pe, ot_done, i - 1)
                    mm(proj_ps, ot[s % 2][:, :], wo[:, :], start=True, stop=True).then_inc(proj_mm, 1)
                if known(i - 3, 0, BATCHES):
                    mm(gate_ps, xn2ts[(s - 3) % 2][:, :], gate_w[:, :], start=True, stop=True).then_inc(gate_mm, 1)
                if known(b, 0, BATCHES):
                    weigh(2)
                    weigh(3)
                    wait(pe, recip_done, b + 1)
                    tr(recipt_ps, recip[p][:, :], ident[:, :]).then_inc(recipt_mm, 1)

            steps(pe, step, STEPS_FROM, LOOP_FROM, LOOP_TO, LOOP_TO, 2)

            def shared_up(g):
                pe.wait_ge(xn2t_kept, (g + 1) * SG)
                for c in range(CHUNKS):
                    if g > 0:
                        pe.wait_ge(s_gelu, 4 * (g - 1) + c + 1)
                    mm(bank_s[:, c * 512:(c + 1) * 512], s_up[:, c * P:(c + 1) * P],
                       tok(xn2t, g * SG, SG), start=True, stop=True).then_inc(s_up_mm, 1)

            def shared_down(g):
                pe.wait_ge(s_gelu, 4 * (g + 1))
                if g >= 2:
                    pe.wait_ge(s_added, g - 1)
                for q in range(SG):
                    for c in range(CHUNKS):
                        last = mm(bank_t[g % 2][:, q * P:(q + 1) * P],
                                  s_act[g % 2][:, c * SW + q * P:c * SW + (q + 1) * P],
                                  s_down[:, c * P:(c + 1) * P], start=(c == 0), stop=(c == CHUNKS - 1))
                last.then_inc(s_down_mm, 1)

            def rank(p):
                pe.wait_ge(chosen, p + 1)
                n = PART[p + 1] - PART[p]
                width = (n + 1) * EXPERTS
                mm(rank_ps[:, 0:width], tri_b[:, :], both[p][:, 0:width], start=True, stop=False)
                for d in range(1, n + 1):
                    last = mm(rank_ps[:, d * EXPERTS:width], ones[:, :], both[p][:, 0:width - d * EXPERTS],
                              start=False, stop=(d == n))
                last.then_inc(rank_mm, 1)

            pe.wait_ge(shared_in, N_SHARED)
            pe.wait_ge(clip_done, 2 * LOOP_TO)
            shared_up(0)
            shared_up(1)
            pe.wait_ge(gate_done, LOOP_TO - 3)
            pe.wait_ge(x1_done, LOOP_TO - 2)
            pe.wait_ge(v_done, LOOP_TO)
            pe.wait_ge(qm_done, LOOP_TO + 1)
            pe.wait_ge(xn1t_done, LOOP_TO + 2)
            rank(0)
            pe.wait_ge(probst_done, 4 * (LOOP_TO - 1))
            shared_down(0)
            shared_down(1)
            pe.wait_ge(ranks_read, 1)
            pe.wait_ge(s_gelu, 4 * MIDDLE)
            for i in range(LOOP_TO, BATCHES):
                step(i, i, 0)
            pe.wait_ge(clip_done, 2 * BATCHES)
            shared_up(2)
            step(BATCHES, BATCHES, 0)
            step(BATCHES + 1, BATCHES + 1, 0)
            shared_up(3)
            step(BATCHES + 2, BATCHES + 2, 0)
            pe.wait_ge(probst_done, 4 * BATCHES)
            shared_down(2)
            pe.wait_ge(gate_done, BATCHES)
            rank(1)
            shared_up(4)
            shared_down(3)
            shared_down(4)

            pe.wait_ge(ranks_read, PARTS)
            pe.wait_ge(ot_done, BATCHES)
            pe.wait_ge(s_gelu, 4 * FRONT)
            pe.wait_ge(s_added, FRONT)

            def routed(j, s, t):
                b, p = j + 1, (s + 1) % 2
                if known(b, 0, TILES):
                    pe.wait_ge(xs_in[(s + 1) % RING], (use_of(s + 1, t) + 1) * 16)
                    wait(pe, xst_done, b - 1)
                    tr((bank_a, bank_b)[p][:, 0:P], xs[(s + 1) % RING][:, :], ident[:, :]).then_inc(xst_mm, 1)
                b, p = j, s % 2
                if known(b, 0, TILES):
                    wait(pe, xst_done, b + 1)
                    wait(pe, up_w_done, b + 1)
                    wait(pe, gelu_done, b - 1)
                    for c in range(CHUNKS):
                        last = mm(bank_s[:, p * 512 + c * P:p * 512 + (c + 1) * P], st_up[p][:, c * P:(c + 1) * P],
                                  xst[p][:, :], start=True, stop=True)
                    last.then_inc(up_mm, 1)
                b, p = j - 1, (s - 1) % 2
                if known(b, 0, TILES):
                    wait(pe, gelu_done, b + 1)
                    wait(pe, down_w_done, b + 1)
                    wait(pe, y_done, b - 1)
                    w = st_down[(s - 1) % RING]
                    for c in range(CHUNKS):
                        last = mm(bank_t[p][:, 0:P], act[p][:, c * P:(c + 1) * P], w[:, c * P:(c + 1) * P],
                                  start=(c == 0), stop=(c == CHUNKS - 1))
                    last.then_inc(down_mm, 1)

            steps(pe, routed, -1, 3, loop_end(3, TILES - 1, TURN), TILES + 1, TURN)

            pe.wait_ge(gelu_done, TILES)
            shared_up(FRONT)
            pe.wait_ge(y_done, TILES)
            for g in range(FRONT + 1, SGROUPS):
                shared_up(g)
                shared_down(g - 1)
            shared_down(SGROUPS - 1)

        @block.scalar
        def _(sc_):
            act_ = nc.scalar.activation

            def step(i, s, t):
                def exps(b, p, heads):
                    if not known(b, 0, BATCHES):
                        return
                    for h in heads:
                        if h == 0:
                            wait(sc_, probst_mm, 4 * (b - 1))
                            wait(sc_, rsum_done, b - 1)
                        if h % (HEADS // 2) == 0:
                            wait(sc_, max_done, 2 * b + 2 * h // HEADS + 1)
                        ins = act_(probs[p][:, h * P:(h + 1) * P], clipped[p][:, h * P:(h + 1) * P], ACT.Exp,
                                   bias=negmax[p][:, h:h + 1], accum_out=sums[p][:, h:h + 1])
                        if h % PER == PER - 1:
                            ins.then_inc(exp_done, 1)

                def evacuate(g):
                    b = i - 1
                    if known(b, 0, BATCHES):
                        wait(sc_, probst_mm, 4 * b + g + 1)
                        wait(sc_, pv_mm, 4 * b + g - 1)
                        nc.scalar.copy(probst[g % 2][:, :], bank_t[g % 2][:, :]).then_inc(probst_done, 1)

                exps(i - 1, (s - 1) % 2, range(EARLY, HEADS))
                evacuate(0)
                evacuate(1)
                if known(i + 2, 0, BATCHES):
                    wait(sc_, xn1t_mm, i + 3)
                if known(i - 3, 0, BATCHES):
                    wait(sc_, xn2t_mm, i - 2)
                    wait(sc_, gate_mm, i - 4)
                    wait(sc_, xn2t_kept, i - 4)
                    nc.scalar.copy(xn2ts[(s - 3) % 2][:, :], xn2t_ps).then_inc(xn2t_done, 1)
                if known(i + 2, 0, BATCHES):
                    wait(sc_, kvq_mm, i + 1)
                    nc.scalar.copy(xn1t[s % 2][:, :], xn1t_ps).then_inc(xn1t_done, 1)
                evacuate(2)
                exps(i, s % 2, range(0, EARLY))
                evacuate(3)

            steps(sc_, step, STEPS_FROM, LOOP_FROM, LOOP_TO, LOOP_TO, 2)

            def shared(g):
                p = g % 2
                for c in range(CHUNKS):
                    sc_.wait_ge(s_up_mm, 4 * g + c + 1)
                    if c == 0 and g >= 2:
                        sc_.wait_ge(s_down_mm, g - 1)
                    act_(s_act[p][:, c * SW:(c + 1) * SW], bank_s[:, c * 512:(c + 1) * 512], ACT.Gelu,
                         bias=s_upb[:, c:c + 1]).then_inc(s_gelu, 1)

            def sigmoid(p):
                lo, hi = PART[p] * EXPERTS, PART[p + 1] * EXPERTS
                sc_.wait_ge(gate_done, PART[p + 1])
                act_(sig[:, lo:hi], logits[:, lo:hi], ACT.Sigmoid).then_inc(sig_done, 1)

            sigmoid(0)
            sc_.wait_ge(shared_in, N_SHARED)
            for g in range(MIDDLE):
                shared(g)
            for i in range(LOOP_TO, BATCHES + 1):
                step(i, i, 0)
            shared(2)
            step(BATCHES + 1, BATCHES + 1, 0)
            step(BATCHES + 2, BATCHES + 2, 0)
            sigmoid(1)
            shared(3)
            shared(4)

            def routed(j, s, t):
                p = s % 2
                wait(sc_, up_mm, j + 1)
                wait(sc_, down_mm, j - 1)
                for c in range(CHUNKS):
                    ins = act_(act[p][:, c * P:(c + 1) * P], bank_s[:, p * 512 + c * P:p * 512 + (c + 1) * P], ACT.Gelu,
                               bias=st_up[p][:, HIDDEN + c:HIDDEN + c + 1])
                ins.then_inc(gelu_done, 1)

            steps(sc_, routed, 0, 2, loop_end(2, TILES, TURN), TILES, TURN)
            for g in range(FRONT, SGROUPS):
                shared(g)

        @block.vector
        def _(dve):
            V = nc.vector
            own = [bass.AP(v[:, :].tensor, v[:, :].offset, [v[:, :].ap[0], [P + HD, HEADS], [1, HD]]) for v in val]
            dve.wait_ge(consts_in, N_CONSTS)
            dve.wait_ge(fills, 5)

            def step(i, s, t):
                b, p = i - 2, s % 2
                if known(b, 0, BATCHES):
                    wait(dve, recipt_mm, b + 1)
                    wait(dve, ot_done, b - 1)
                    V.tensor_copy(recipt[p][:, :], recipt_ps).then_inc(recipt_done, 1)
                    wait(dve, recipt_done, b + 1)
                    wait(dve, proj_mm, b - 1)
                wait(dve, stat2_done, min(i - 2, BATCHES) if isinstance(i, int) else i - 2)
                wait(dve, xn2_done, i - 4)
                if known(b, 0, BATCHES):
                    V.tensor_tensor(ot[p][:, :], ot_ps, recipt[p][:, :], ALU.mult).then_inc(ot_done, 1)
                if known(i - 3, 0, BATCHES):
                    p = (s - 3) % 2
                    V.bn_aggr(mv2[p][:, :], stat2[p][:, :]).then_inc(mv2_done, 1)
                b, p = i, s % 2
                if known(b, 0, BATCHES):
                    wait(dve, kvq_mm, b + 2)
                    wait(dve, pv_mm, 4 * (b - 1))
                    V.tensor_tensor(own[p],
                                    kv_v.rearrange("p (h d) -> p h d", d=HD),
                                    bv[:, :].rearrange("p (h d) -> p h d", d=HD), ALU.add).then_inc(v_done, 1)
                b, p = i + 1, (s + 1) % 2
                if known(b, 0, BATCHES):
                    wait(dve, kvq_mm, b + 1)
                    wait(dve, scores_mm, 2 * (b - 1))
                    for dst, src, bias, mask, n, done in ((km, kv_k, bk, kmask, PER, km_done),
                                                          (qm, kv_q, bq, qmask, GROUPS, qm_done)):
                        if done is qm_done:
                            wait(dve, mv1_done, i + 2)
                        V.scalar_tensor_tensor(dst[p][:, :].rearrange("p (n k) -> p n k", k=P),
                                               src.unsqueeze(1).to_broadcast([P, n, P]), bias[:, 0:1],
                                               mask[:, :].unsqueeze(2).to_broadcast([P, n, P]),
                                               op0=ALU.add, op1=ALU.mult).then_inc(done, 1)
                b, p = i + 3, (s + 3) % 2
                if known(b, 0, BATCHES):
                    if isinstance(b, int):
                        dve.wait_ge(x_in[b * XCHUNKS // BATCHES], 16)
                        wait(dve, mv1_done, b - 1)
                    elif s == LOOP_FROM:
                        for c in range(1, XCHUNKS):
                            dve.wait_ge(x_in[c], 16)
                    V.bn_stats(stat1[p][:, :], tok(x, b)).then_inc(stat1_done, 1)
                    wait(dve, stat1_done, b + 1)
                    wait(dve, xn1_done, b - 1)
                b, p = i + 2, s % 2
                if known(b, 0, BATCHES):
                    wait(dve, rstd1_done, b + 1)
                    wait(dve, xn1t_mm, b - 1)
                    V.tensor_scalar(xn1[p][:, :], tok(x, b), mv1[p][:, 0:1], rstd1[p][:, 0:1],
                                    ALU.subtract, ALU.mult).then_inc(xn1_done, 1)
                if known(i + 3, 0, BATCHES):
                    p = (s + 3) % 2
                    V.bn_aggr(mv1[p][:, :], stat1[p][:, :]).then_inc(mv1_done, 1)
                b, p = i - 3, (s - 3) % 2
                if known(b, 0, BATCHES):
                    wait(dve, rstd2_done, b + 1)
                    wait(dve, xn2t_mm, b - 1)
                    wait(dve, xn2_kept, b - 1)
                    V.tensor_scalar(xn2s[p][:, :], tok(x, b), mv2[p][:, 0:1], rstd2[p][:, 0:1],
                                    ALU.subtract, ALU.mult).then_inc(xn2_done, 1)
                b, p = i, s % 2
                if known(b, 0, BATCHES):
                    wait(dve, max_done, 2 * (b - 1))
                    wait(dve, exp_done, 4 * (b - 1))
                    for half in range(2):
                        at, n = half * HEADS // 2, HEADS // 2
                        wait(dve, scores_mm, 2 * b + half + 1)
                        V.tensor_scalar(clipped[p][:, at * P:(at + n) * P], bank_s[:, at * P:(at + n) * P],
                                        -CLAMP, CLAMP, ALU.max, ALU.min).then_inc(clip_done, 1)
                        wait(dve, clip_done, 2 * b + half + 1)
                        V.tensor_reduce(negmax[p][:, at:at + n],
                                        clipped[p][:, at * P:(at + n) * P].rearrange("p (h k) -> p h k", k=P), AX.X,
                                        ALU.max, negate=True).then_inc(max_done, 1)
                b, p = i - 1, (s - 1) % 2
                if known(b, 0, BATCHES):
                    wait(dve, exp_done, 4 * (b + 1))
                    wait(dve, recip_done, b - 1)
                    V.reciprocal(rsum[p][:, :], sums[p][:, :]).then_inc(rsum_done, 1)
                    wait(dve, rsum_done, b + 1)
                    wait(dve, recipt_mm, b - 1)
                    V.tensor_copy(recip[p][:, :].rearrange("p (h d) -> p h d", d=HD),
                                  rsum[p][:, :].unsqueeze(2).to_broadcast([P, HEADS, HD])).then_inc(recip_done, 1)
                b, p = i - 2, s % 2
                if known(b, 0, BATCHES):
                    wait(dve, proj_mm, b + 1)
                    if known(b - 1, 0, BATCHES):
                        wait(dve, gate_mm, b)
                    wait(dve, xb_done, b + 1)
                    V.tensor_tensor(tok(x, b), proj_ps, xb[p][:, :], ALU.add).then_inc(x1_done, 1)
                    wait(dve, x1_done, b + 1)
                    wait(dve, mv2_done, b - 1)
                b = i - 3
                if known(b, 0, BATCHES):
                    wait(dve, gate_mm, b + 1)
                    dst = logits[:, b * EXPERTS:(b + 1) * EXPERTS] if isinstance(b, int) else logits[:, bass.ds(b * EXPERTS, EXPERTS)]
                    V.tensor_tensor(dst, gate_ps, gate_b[:, :], ALU.add).then_inc(gate_done, 1)
                if known(i - 2, 0, BATCHES):
                    V.bn_stats(stat2[s % 2][:, :], tok(x, i - 2)).then_inc(stat2_done, 1)

            steps(dve, step, STEPS_FROM, LOOP_FROM, LOOP_TO, LOOP_TO, 2)

            def add_shared(g):
                xg = tok(x, g * SG, SG)
                V.tensor_tensor(xg.rearrange("p (b c) -> p b c", c=P), xg.rearrange("p (b c) -> p b c", c=P),
                                s_downb01[:, :].unsqueeze(1).to_broadcast([P, SG, P]), ALU.add).then_inc(s_bias, 1)
                dve.wait_ge(s_bias, g + 1)
                dve.wait_ge(s_down_mm, g + 1)
                V.scalar_tensor_tensor(xg, bank_t[g % 2][:, :], 0.1, xg, op0=ALU.mult, op1=ALU.add).then_inc(s_added, 1)

            count_of = [0]

            def do(ins):
                count_of[0] += 1
                ins.then_inc(route, 1)
                dve.wait_ge(route, count_of[0])

            def choose(p):
                lo, hi = PART[p], PART[p + 1]

                def flat(t):
                    return t[:, lo * EXPERTS:hi * EXPERTS]

                def tiles(t):
                    return by_e(t)[:, lo:hi, :]

                def per_e(t):
                    return t[:, lo:hi].unsqueeze(2).to_broadcast([P, hi - lo, EXPERTS])

                dve.wait_ge(sig_done, p + 1)
                for k, scores in enumerate((sig, sig2)):
                    do(V.tensor_reduce(best[k][:, lo:hi], tiles(scores), AX.X, ALU.max))
                    do(V.tensor_tensor(tiles(eq), tiles(scores), per_e(best[k]), ALU.is_equal))
                    do(V.tensor_tensor(tiles(sc), tiles(eq),
                                       rank_w.unsqueeze(1).to_broadcast([P, hi - lo, EXPERTS]), ALU.mult))
                    do(V.tensor_reduce(win[:, lo:hi], tiles(sc), AX.X, ALU.max))
                    do(V.tensor_tensor(tiles(oh[k]), tiles(sc), per_e(win), ALU.is_equal))
                    if k == 0:
                        do(V.scalar_tensor_tensor(flat(sig2), flat(oh[0]), -4.0, flat(sig), op0=ALU.mult, op1=ALU.add))
                width = (hi - lo) * EXPERTS
                do(V.memset(both[p][:, width:width + EXPERTS], 0.0))
                V.tensor_tensor(both[p][:, 0:width], flat(oh[0]), flat(oh[1]), ALU.add).then_inc(chosen, 1)
                do(V.scalar_tensor_tensor(den[:, lo:hi], best[0][:, lo:hi], 1e-6, best[1][:, lo:hi],
                                          op0=ALU.add, op1=ALU.add))
                do(V.reciprocal(rden[:, lo:hi], den[:, lo:hi]))
                for k in range(TOPK):
                    do(V.tensor_tensor(weight[k][:, lo:hi], best[k][:, lo:hi], rden[:, lo:hi], ALU.mult))

            def place(p):
                lo, hi, width = PART[p], PART[p + 1], (PART[p + 1] - PART[p]) * EXPERTS

                def flat(t):
                    return t[:, lo * EXPERTS:hi * EXPERTS]

                dve.wait_ge(rank_mm, p + 1)
                V.tensor_copy(ranks[:, 0:width + EXPERTS], rank_ps[:, 0:width + EXPERTS]).then_inc(ranks_read, 1)
                dve.wait_ge(ranks_read, p + 1)
                if p == 1:
                    add_shared(MIDDLE)
                count = ranks[:, width:width + EXPERTS]
                do(V.tensor_scalar(count_i[:, :], count, float(P - 1), None, ALU.add))
                do(V.tensor_scalar(count_j[:, :], count_i[:, :], 7, 7, ALU.logical_shift_right, ALU.logical_shift_left))
                do(V.tensor_copy(padded[:, :], count_j[:, :]))
                src, dst, d = padded, base_a, 1
                while d < EXPERTS:
                    do(V.tensor_copy(dst[:, 0:d], src[:, 0:d]))
                    do(V.tensor_tensor(dst[:, d:EXPERTS], src[:, d:EXPERTS], src[:, 0:EXPERTS - d], ALU.add))
                    src, dst, d = dst, (base_b if dst is base_a else base_a), 2 * d
                ends = src
                do(V.tensor_tensor(starts[:, :], ends[:, :], padded[:, :], ALU.subtract))
                do(V.tensor_tensor(by_e(sig2)[:, lo:hi, :], by_e(ranks)[:, 0:hi - lo, :],
                                   starts[:, :].unsqueeze(1).to_broadcast([P, hi - lo, EXPERTS]), ALU.add))
                for k in range(TOPK):
                    do(V.tensor_tensor(flat(sc), flat(sig2), flat(oh[k]), ALU.mult))
                    do(V.tensor_reduce(slot_f[k][:, lo:hi], by_e(sc)[:, lo:hi, :], AX.X, ALU.add))
                    do(V.tensor_copy(slot[k][:, lo:hi], slot_f[k][:, lo:hi]))
                V.tensor_copy(flat(eq)[:, 1:2], ends[:, 0:1]).then_inc(slots_done, 1)
                lo, hi = PTILE[p], PTILE[p + 1]
                do(V.tensor_tensor(by_e(passed)[:, lo:hi, :],
                                   ends[:, :].unsqueeze(1).to_broadcast([P, hi - lo, EXPERTS]),
                                   tile_at[:, lo:hi].unsqueeze(2).to_broadcast([P, hi - lo, EXPERTS]), ALU.is_le))
                do(V.tensor_reduce(expert_f[:, lo:hi], by_e(passed)[:, lo:hi, :], AX.X, ALU.add))
                do(V.tensor_scalar(expert_g[:, lo:hi], expert_f[:, lo:hi], float(EXPERTS - 1), None, ALU.min))
                do(V.tensor_copy(expert[:, lo:hi], expert_g[:, lo:hi]))

            dve.wait_ge(shared_in, N_SHARED)
            do(V.tensor_scalar(s_downb01[:, :], s_downb[:, :], 0.1, None, ALU.mult))
            do(V.tensor_copy(tri_b[:, :], tri))
            choose(0)
            place(0)
            for g in range(MIDDLE):
                add_shared(g)
            for i in range(LOOP_TO, STEPS_TO):
                step(i, i, 0)
            choose(1)
            place(1)
            for g in range(MIDDLE + 1, FRONT):
                add_shared(g)
            dve.wait_ge(ffn_in, N_FFN)

            def routed(j, s, t):
                b = j + 1
                if known(b, 0, TILES):
                    at = expert[0:1, b:b + 1] if isinstance(b, int) else expert[0:1, bass.ds(b, 1)]
                    its_expert = V.value_load(at, min_val=0, max_val=EXPERTS - 1)
                b, p = j - 2, s % 2
                if known(b, 0, TILES):
                    n = (s - 2) % RING
                    wait(dve, down_mm, b + 1)
                    if not isinstance(b, int) or b >= RING:
                        dve.wait_ge(y_out[n], use_of(s - 2, t) * 16)
                    V.tensor_tensor(y[n][:, :], bank_t[p][:, 0:P], st_down[n][:, HIDDEN:DNW],
                                    ALU.add).then_inc(y_done, 1)
                b, p = j + 1, (s + 1) % 2
                if known(b, 0, TILES):
                    wait(dve, xst_mm, b + 1)
                    wait(dve, up_mm, b - 1)
                    V.tensor_copy(xst[p][:, :], (bank_a, bank_b)[p][:, 0:P]).then_inc(xst_done, 1)
                    wait(dve, gelu_done, b - 1)
                    V.tensor_copy(st_up[p][:, :], up_w[:, bass.ds(its_expert * UPW, UPW)]).then_inc(up_w_done, 1)
                    wait(dve, y_done, b - RING + 1)
                    V.tensor_copy(st_down[(s + 1) % RING][:, :],
                                  down_w[:, bass.ds(its_expert * DNW, DNW)]).then_inc(down_w_done, 1)

            steps(dve, routed, -1, 7, loop_end(7, TILES - 1, TURN), TILES + 2, TURN)

            def add_first(t):
                if t % YGROUP == 0:
                    dve.wait_ge(y_in[t // YGROUP], 16 * TOPK * YGROUP)
                if t >= 2:
                    dve.wait_ge(summed, t - 1)
                V.scalar_tensor_tensor(part[t % 2][:, :], gathered(0, t), weight[0][:, t:t + 1], tok(x, t),
                                       op0=ALU.mult, op1=ALU.add).then_inc(half_sum, 1)

            def add_second(t):
                dve.wait_ge(half_sum, t + 1)
                V.scalar_tensor_tensor(tok(x, t), gathered(1, t), weight[1][:, t:t + 1], part[t % 2][:, :],
                                       op0=ALU.mult, op1=ALU.add).then_inc(summed, 1)

            for g in range(SGROUPS):
                if g >= FRONT:
                    add_shared(g)
                    dve.wait_ge(s_added, g + 1)
                for t in range(g * SG, (g + 1) * SG, 2):
                    add_first(t)
                    add_first(t + 1)
                    add_second(t)
                    add_second(t + 1)


def kernel(x, ctx_768, L0_xattn_Wq, L0_xattn_bq, L0_xattn_Wk, L0_xattn_bk, L0_xattn_Wv, L0_xattn_bv,
           L0_xattn_Wo, L0_xattn_bo, L0_ffn_gate_w, L0_ffn_gate_bias, L0_ffn_Wu, L0_ffn_bu, L0_ffn_Wd,
           L0_ffn_bd, L0_ffn_sWu, L0_ffn_sbu, L0_ffn_sWd, L0_ffn_sbd):
    import concourse.bacc as bacc
    import numpy as np
    from concourse.bass_utils import run_bass_kernel_spmd

    def rows_of(w):
        w = np.asarray(w)
        w = w.reshape(w.shape[:-1] + (CHUNKS, P))
        order = (w.ndim - 1,) + tuple(range(w.ndim - 3)) + (w.ndim - 2, w.ndim - 3)
        return w.transpose(order)

    def packed(parts, arrays_of):
        values = [np.atleast_2d(np.asarray(arrays_of[name])) for name, _ in parts]
        whole = np.zeros((max(v.shape[0] for v in values), sum(w for _, w in parts)), np.float32)
        at = 0
        for v, (_, w) in zip(values, parts):
            whole[:v.shape[0], at:at + w] = v
            at += w
        return whole

    part = np.arange(P)
    data = {
        "x": x,
        "ctxt": np.asarray(ctx_768).transpose(2, 0, 1).reshape(CTX, TOKENS),
        "cols": packed(COLS, {
            "wq": L0_xattn_Wq, "wk": L0_xattn_Wk, "wv": L0_xattn_Wv, "wo": L0_xattn_Wo,
            "gate_w": np.asarray(L0_ffn_gate_w).transpose(1, 0), "ident": np.eye(P),
            "tri": np.triu(np.ones((P, P)), 1),
            "qmask": (part[:, None] // (P // GROUPS) == np.arange(GROUPS)) * HD ** -0.5,
            "kmask": part[:, None] // HD % PER == np.arange(PER),
            "bq": np.asarray(L0_xattn_bq).reshape(P, 1), "bk": np.asarray(L0_xattn_bk).reshape(P, 1)}),
        "rows": packed(ROWS, {
            "bv": L0_xattn_bv, "bo": L0_xattn_bo, "gate_b": L0_ffn_gate_bias,
            "rank_w": np.arange(EXPERTS, 0, -1), "tile_at": np.concatenate([np.arange(PTILE[p + 1] - PTILE[p]) for p in range(PARTS)]) * P})[0],
        "up": np.concatenate([np.asarray(L0_ffn_Wu).transpose(2, 0, 1),
                              np.asarray(L0_ffn_bu).reshape(EXPERTS, CHUNKS, P).transpose(2, 0, 1)],
                             axis=2).reshape(P, EXPERTS * UPW),
        "down": rows_of(L0_ffn_Wd).reshape(P, EXPERTS * HIDDEN),
        "downb": L0_ffn_bd,
        "s_up": np.asarray(L0_ffn_sWu).transpose(1, 0),
        "s_upb": np.asarray(L0_ffn_sbu).reshape(CHUNKS, P).transpose(1, 0),
        "s_down": rows_of(L0_ffn_sWd).reshape(P, HIDDEN),
        "s_downb": L0_ffn_sbd,
    }
    nc = bacc.Bacc("TRN2", target_bir_lowering=False, num_devices=1)
    arrays, dr = {}, {}
    for name, a in data.items():
        arrays[f"in_{name}"] = np.ascontiguousarray(a)
        dr[name] = nc.dram_tensor(f"in_{name}", arrays[f"in_{name}"].shape, F32, kind="ExternalInput").ap()
    out = nc.dram_tensor("out_dram", (BATCHES, P, P), F32, kind="ExternalOutput").ap()
    xattn_moe(nc, dr, out)
    return run_bass_kernel_spmd(nc, [arrays], core_ids=[0]).results[0]["out_dram"]
```
